# Optimizing a Trainium2 kernel written in Bass

```python
import numpy as np
import jax
import jax.numpy as jnp

def _softmax(x, axis=-1):
    return jax.nn.softmax(x, axis=axis)

def _gelu(x):
    return jax.nn.gelu(x, approximate=True)

def _silu(x):
    return jax.nn.silu(x)

def _sigmoid(x):
    return jax.nn.sigmoid(x)

def _layernorm(x, axis=-1, eps=1e-05):
    m = jnp.mean(x, axis=axis, keepdims=True)
    v = jnp.var(x, axis=axis, keepdims=True)
    return (x - m) / jnp.sqrt(v + eps)

def _scatter_add(tgt, idx, src, axis=0):
    return tgt.at[idx].add(src)

def _segment_sum(src, seg, n):
    return jax.ops.segment_sum(src, seg, n)
kernel_name = 'mk_decoder_postln_d1_seqx_r8_c9b5de'

def setup_inputs(seed: int=0):
    np.random.seed(seed)
    _w = jnp.asarray

    def _rec_inputs():
        import jax
        import jax.numpy as jnp
        _rk = jax.random.key(seed)
        x = -0.0002928 + 1 * jax.random.normal(jax.random.fold_in(_rk, 1), (2, 512, 128), jnp.float32)
        _lenS = 512 - jax.random.randint(jax.random.fold_in(_rk, 7), (2,), 0, max(1, 512 // 4) + 1, jnp.int32)
        _lenS2 = 32 - jax.random.randint(jax.random.fold_in(_rk, 8), (2,), 0, max(1, 32 // 4) + 1, jnp.int32)
        _ctx_1024P = jax.random.normal(jax.random.fold_in(_rk, 11), (2, 16, 128), jnp.float32)
        _ctx_1024c = jax.random.dirichlet(jax.random.fold_in(_rk, 511), 0.3 * jnp.ones((16,), jnp.float32), (2, 32))
        _ctx_1024t = jnp.einsum('bsk,bkd->bsd', _ctx_1024c, _ctx_1024P)
        _ctx_1024t = _ctx_1024t * jax.lax.rsqrt(jnp.mean(jnp.square(_ctx_1024t)) + 1e-12) * 0.953939
        ctx_1024 = 0.00222621 + 0.99962 * (_ctx_1024t + 0.3 * jax.random.normal(jax.random.fold_in(_rk, 611), (2, 32, 128), jnp.float32))
        return (x, ctx_1024)
    x, ctx_1024 = _rec_inputs()

    def _L0_attn_setup():
        import jax, jax.numpy as jnp
        import numpy as np
        B, S, E, H, P = (2, 256, 128, 16, 256)
        HD = E // H
        key = jax.random.key(seed)
        ks = jax.random.split(key, 10)
        std = E ** (-0.5)
        x = jax.random.normal(ks[0], (B, S, E), jnp.float32)
        Wq = jax.random.normal(ks[1], (E, E), jnp.float32) * std
        Wk = jax.random.normal(ks[2], (E, E), jnp.float32) * std
        Wv = jax.random.normal(ks[3], (E, E), jnp.float32) * std
        Wo = jax.random.normal(ks[4], (E, E), jnp.float32) * std
        rel_key = jax.random.normal(ks[5], (P, HD), jnp.float32) * 0.02
        z = jnp.zeros((E,), jnp.float32)
        return {'x': x, 'Wq': Wq, 'bq': z, 'Wk': Wk, 'bk': z, 'Wv': Wv, 'bv': z, 'Wo': Wo, 'bo': z, 'rel_key': rel_key}
    _L0_attn_all = _L0_attn_setup()
    _L0_attn_in = {k: v for k, v in _L0_attn_all.items() if k in ('Wq', 'bq', 'Wk', 'bk', 'Wv', 'bv', 'Wo', 'bo', 'rel_key')}
    del _L0_attn_all

    def _L0_xattn_setup():
        import jax, jax.numpy as jnp
        import numpy as np
        DIM = 128
        HEADS = 16
        DIM_HEAD = 64
        INNER = HEADS * DIM_HEAD
        EPS = 1e-05

        def _split_heads(t):
            b, n, _ = t.shape
            return t.reshape(b, n, HEADS, DIM_HEAD).transpose(0, 2, 1, 3)
        key = jax.random.key(seed)
        ks = jax.random.split(key, 9)
        b, n, m = (2, 256, 32)
        s = DIM ** (-0.5)
        return {'x': jax.random.normal(ks[0], (b, n, DIM), jnp.float32), 'memories': jax.random.normal(ks[1], (b, m, DIM), jnp.float32), 'ln_g': jnp.ones((DIM,), jnp.float32), 'ln_b': jnp.zeros((DIM,), jnp.float32), 'Wq': jax.random.normal(ks[2], (DIM, INNER), jnp.float32) * s, 'Wkv': jax.random.normal(ks[3], (DIM, 2 * INNER), jnp.float32) * s, 'Wm': jax.random.normal(ks[4], (DIM, INNER), jnp.float32) * s, 'Wo': jax.random.normal(ks[5], (INNER, DIM), jnp.float32) * s, 'bo': jnp.zeros((DIM,), jnp.float32)}
    _L0_xattn_all = _L0_xattn_setup()
    _L0_xattn_in = {k: v for k, v in _L0_xattn_all.items() if k in ('ln_g', 'ln_b', 'Wq', 'Wkv', 'Wm', 'Wo', 'bo')}
    del _L0_xattn_all

    def _L0_ffn_setup():
        import jax, jax.numpy as jnp
        import numpy as np
        H = 128
        E = 8
        B, S = (4, 256)
        key = jax.random.key(seed)
        k1, k2, k3, k4 = jax.random.split(key, 4)
        x = jax.random.normal(k1, (B, S, H), dtype=jnp.float32)
        wg = jax.random.normal(k2, (H, E), dtype=jnp.float32) * 0.02
        W = jax.random.normal(k3, (E, H, H), dtype=jnp.float32) * 0.02
        b = jax.random.normal(k4, (E, H), dtype=jnp.float32) * 0.02
        return {'x': x, 'wg': wg, 'W': W, 'b': b}
    _L0_ffn_all = _L0_ffn_setup()
    _L0_ffn_in = {k: v for k, v in _L0_ffn_all.items() if k in ('wg', 'W', 'b')}
    del _L0_ffn_all
    return {'x': x, 'ctx_1024': ctx_1024, 'L0_attn_Wq': _L0_attn_in['Wq'], 'L0_attn_bq': _L0_attn_in['bq'], 'L0_attn_Wk': _L0_attn_in['Wk'], 'L0_attn_bk': _L0_attn_in['bk'], 'L0_attn_Wv': _L0_attn_in['Wv'], 'L0_attn_bv': _L0_attn_in['bv'], 'L0_attn_Wo': _L0_attn_in['Wo'], 'L0_attn_bo': _L0_attn_in['bo'], 'L0_attn_rel_key': _L0_attn_in['rel_key'], 'L0_xattn_ln_g': _L0_xattn_in['ln_g'], 'L0_xattn_ln_b': _L0_xattn_in['ln_b'], 'L0_xattn_Wq': _L0_xattn_in['Wq'], 'L0_xattn_Wkv': _L0_xattn_in['Wkv'], 'L0_xattn_Wm': _L0_xattn_in['Wm'], 'L0_xattn_Wo': _L0_xattn_in['Wo'], 'L0_xattn_bo': _L0_xattn_in['bo'], 'L0_ffn_wg': _L0_ffn_in['wg'], 'L0_ffn_W': _L0_ffn_in['W'], 'L0_ffn_b': _L0_ffn_in['b']}

def reference(x, ctx_1024, L0_attn_Wq, L0_attn_bq, L0_attn_Wk, L0_attn_bk, L0_attn_Wv, L0_attn_bv, L0_attn_Wo, L0_attn_bo, L0_attn_rel_key, L0_xattn_ln_g, L0_xattn_ln_b, L0_xattn_Wq, L0_xattn_Wkv, L0_xattn_Wm, L0_xattn_Wo, L0_xattn_bo, L0_ffn_wg, L0_ffn_W, L0_ffn_b):
    import jax
    import jax.numpy as jnp

    def _L0_attn_ref(x, Wq, bq, Wk, bk, Wv, bv, Wo, bo, rel_key):
        import jax, jax.numpy as jnp
        import numpy as np
        B, S, E, H, P = (2, 256, 128, 16, 256)
        HD = E // H
        b, s, e = x.shape
        p, hd = rel_key.shape
        h = e // hd
        scale = hd ** (-0.5)

        def split_heads(t):
            return t.reshape(b, s, h, hd).transpose(0, 2, 1, 3)
        q = split_heads(x @ Wq + bq)
        k = split_heads(x @ Wk + bk)
        v = split_heads(x @ Wv + bv)
        scores = jnp.einsum('bhid,bhjd->bhij', q, k)
        rel = jnp.einsum('bhid,pd->bhip', q, rel_key)
        i = jnp.arange(s)[:, None]
        j = jnp.arange(s)[None, :]
        rel_idx = jnp.clip(j - i + p - 1, 0, p - 1)
        bias = jnp.take_along_axis(rel, jnp.broadcast_to(rel_idx[None, None], (b, h, s, s)), axis=3)
        causal = j <= i
        logits = jnp.where(causal[None, None], (scores + bias) * scale, -jnp.inf)
        attn = jax.nn.softmax(logits, axis=-1)
        out = jnp.einsum('bhij,bhjd->bhid', attn, v)
        out = out.transpose(0, 2, 1, 3).reshape(b, s, e)
        return out @ Wo + bo

    def _L0_xattn_ref(x, memories, ln_g, ln_b, Wq, Wkv, Wm, Wo, bo):
        import jax, jax.numpy as jnp
        import numpy as np
        DIM = 128
        HEADS = 16
        DIM_HEAD = 64
        INNER = HEADS * DIM_HEAD
        EPS = 1e-05

        def _split_heads(t):
            b, n, _ = t.shape
            return t.reshape(b, n, HEADS, DIM_HEAD).transpose(0, 2, 1, 3)
        mu = jnp.mean(x, axis=-1, keepdims=True)
        var = jnp.mean(jnp.square(x - mu), axis=-1, keepdims=True)
        xn = (x - mu) * jax.lax.rsqrt(var + EPS) * ln_g + ln_b
        q = _split_heads(xn @ Wq)
        kv = xn @ Wkv
        k = _split_heads(kv[..., :INNER])
        v = _split_heads(kv[..., INNER:])
        mem = _split_heads(memories @ Wm)
        k = jnp.concatenate([k, mem], axis=2)
        v = jnp.concatenate([v, mem], axis=2)
        scale = DIM_HEAD ** (-0.5)
        dots = jnp.einsum('bhid,bhjd->bhij', q, k) * scale
        attn = jax.nn.softmax(dots, axis=-1)
        out = jnp.einsum('bhij,bhjd->bhid', attn, v)
        b, h, n, d = out.shape
        out = out.transpose(0, 2, 1, 3).reshape(b, n, h * d)
        return out @ Wo + bo

    def _L0_ffn_ref(x, wg, W, b):
        import jax, jax.numpy as jnp
        import numpy as np
        H = 128
        E = 8
        B, S = (4, 256)
        Bb, Ss, Hh = x.shape
        Ee = wg.shape[1]
        T = Bb * Ss
        C = T // Ee
        xt = x.reshape(T, Hh)
        logits = xt @ wg
        probs = jax.nn.softmax(logits, axis=-1)
        idx = jnp.argmax(probs, axis=-1)
        mask = jax.nn.one_hot(idx, Ee, dtype=xt.dtype)
        locations = jnp.cumsum(mask, axis=0) - mask
        mask = mask * (locations < C).astype(xt.dtype)
        gate = jnp.sum(probs * mask, axis=-1)
        loc_s = jnp.sum(locations * mask, axis=-1).astype(jnp.int32)
        loc_oh = jax.nn.one_hot(loc_s, C, dtype=xt.dtype)
        dispatch = mask[:, :, None] * loc_oh[:, None, :]
        combine = gate[:, None, None] * dispatch
        exp_in = jnp.einsum('tec,th->ech', dispatch, xt)
        exp_out = jnp.einsum('ech,efh->ecf', exp_in, W) + b[:, None, :]
        out = jnp.einsum('tec,ecf->tf', combine, exp_out)
        return out.reshape(Bb, Ss, Hh)
    x = _layernorm(x + _L0_attn_ref(x, L0_attn_Wq, L0_attn_bq, L0_attn_Wk, L0_attn_bk, L0_attn_Wv, L0_attn_bv, L0_attn_Wo, L0_attn_bo, L0_attn_rel_key), axis=-1)
    x = _layernorm(x + _L0_xattn_ref(x, ctx_1024, L0_xattn_ln_g, L0_xattn_ln_b, L0_xattn_Wq, L0_xattn_Wkv, L0_xattn_Wm, L0_xattn_Wo, L0_xattn_bo), axis=-1)
    x = _layernorm(x + _L0_ffn_ref(x, L0_ffn_wg, L0_ffn_W, L0_ffn_b), axis=-1)
    return x

_drawn_inputs = setup_inputs


def setup_inputs(seed=0):
    import zlib

    import numpy as np

    out = dict(_drawn_inputs(seed))
    spreads = {'L0_attn_bq': (0.0, 0.303),
     'L0_attn_bk': (0.0, 0.8),
     'L0_attn_bv': (0.0, 0.1),
     'L0_attn_bo': (0.0, 0.1),
     'L0_xattn_ln_g': (1.0, 0.2),
     'L0_xattn_ln_b': (0.0, 0.1),
     'L0_xattn_bo': (0.0, 0.1)}
    factors = {'L0_attn_rel_key': 8.0, 'L0_ffn_b': 8.0}
    for name, (base, spread) in spreads.items():
        noise = np.random.default_rng([zlib.crc32(name.encode()), seed]).standard_normal(out[name].shape)
        drawn = base * np.exp(spread * noise) if base else spread * noise
        out[name] = jnp.asarray(drawn.astype(out[name].dtype))
    for name, factor in factors.items():
        out[name] = (out[name] * factor).astype(out[name].dtype)
    return out
```

```python
from contextlib import ExitStack

import concourse.bass as bass
from concourse import mybir
from concourse.alu_op_type import AluOpType as ALU

F32 = mybir.dt.float32
BF16 = mybir.dt.bfloat16
ACT = mybir.ActivationFunctionType
AX = mybir.AxisListType

P = 128
NB, S, E = 2, 512, 128
T = S // P
EPS = 1e-5
NEG = -1e30

H, HD, REL = 16, 8, 256
QI = P // H
GI = 32
GT = GI // QI
G = S // GI
WIN = S - QI
TW = WIN + GI
SCALE_A = HD ** -0.5


def chunks(g):
    return -(-GI * (g + 1) // P)


TR0 = [sum(chunks(k) for k in range(g)) for g in range(G + 1)]
NTR = TR0[G]
assert NTR % 4 == 0

XD, M = 64, 32
NP = 8
KEYS = S + M
KH = KEYS // 2
NU = NP * T
SCALE_B = XD ** -0.5

NE, CAP = 8, NB * S // 8
EXPERT_BANKS = (0, 2, 6)
TT = NB * T

LN = 3 * T + 1
N_LOADS_A, N_LOADS_B = 8, 9


def decoder_layer(nc, x, ctx, wq, bq, wk, bk, wv, bv, wo, bo, rel, ln_g, ln_b, xwq, xwkv, xwm, xwo, xbo,
                  wg, we, be, out):
    with ExitStack() as stack:
        def sb(name, shape, dt=F32):
            return stack.enter_context(nc.sbuf_tensor(name, shape, dt))

        def sem(name):
            return stack.enter_context(nc.semaphore(name))

        ident = sb("ident", [P, P])
        ones_row = sb("ones_row", [1, P])
        ones_bf = sb("ones_bf", [P, P], BF16)
        before = sb("before", [P, P], BF16)
        head_mask = sb("head_mask", [P, H])
        quad_mask = sb("quad_mask", [P, 4])
        power = sb("power", [P, TT])
        rank = sb("rank", [P, NE])
        wqkv = sb("wqkv", [P, 3, E])
        wo_sb = sb("wo_sb", [P, E])
        bcols = sb("bcols", [P, 5])
        rows = sb("rows", [1, 3, E])
        rel_sb = sb("rel_sb", [P, REL // P, HD])
        rel_ext = sb("rel_ext", [HD, TW + QI])
        toep = sb("toep", [P, TW])
        xwo_sb = sb("xwo_sb", [P, NP, E])
        ctx_sb = sb("ctx_sb", [NB * M, E])
        ctxT = sb("ctxT", [P, NB * M])
        wg_sb = sb("wg_sb", [P, NE])
        we_sb = sb("we_sb", [P, NE, E])
        weT = sb("weT", [P, NE, E])
        be_sb = sb("be_sb", [NE, E])
        x_sb = sb("x_sb", [P, T, E])
        xT = sb("xT", [P, S])
        qT = sb("qT", [P, S])
        kT = sb("kT", [P, S])
        v_sb = sb("v_sb", [P, T, E])
        q_rep = sb("q_rep", [QI * HD, H, S])
        q_heads = [sb(f"q_heads{k}", [P, GI, H]) for k in range(2)]
        q_pos = [sb(f"q_pos{k}", [P, GI, H]) for k in range(2)]
        prob_a = [sb(f"prob_a{k}", [P, GT, S]) for k in range(2)]
        stat_a = sb("stat_a", [P, 3, 2, GT])
        probT_a = sb("probT_a", [P, T, GT * P])
        o_masked = sb("o_masked", [P, GI, 4])
        outT_a = sb("outT_a", [P, S])
        z = sb("z", [P, TT, E])
        stats = sb("stats", [P, TT, 6])
        moments = sb("moments", [P, TT, 2])
        var_eps = sb("var_eps", [P, TT])
        rstd = sb("rstd", [P, TT])
        x1 = sb("x1", [P, T, E])
        x1n = sb("x1n", [P, T, E])
        x2 = sb("x2", [P, TT, E])
        w_pair = [sb(f"w_pair{k}", [P, 4, P]) for k in range(2)]
        xnT = sb("xnT", [P, S])
        ctxT_b = sb("ctxT_b", [P, M])
        q_pair = [sb(f"q_pair{k}", [P, S]) for k in range(2)]
        k_head = [[sb(f"k_head{k}{h}", [P, KEYS]) for h in range(2)] for k in range(2)]
        v_pair = [sb(f"v_pair{k}", [P, T, P]) for k in range(2)]
        vm_pair = [sb(f"vm_pair{k}", [M, P]) for k in range(2)]
        prob_b = [sb(f"prob_b{h}", [P, KEYS]) for h in range(2)]
        stat_b = sb("stat_b", [P, 3, 2])
        probT_b = [sb(f"probT_b{h}", [P, T, P]) for h in range(2)]
        probTm = sb("probTm", [M, 2, P])
        outT_b = sb("outT_b", [P, NP, S])
        x2T = sb("x2T", [P, TT * P])
        lg = sb("lg", [P, TT, NE])
        ex = sb("ex", [P, TT, NE])
        cand = sb("cand", [P, TT, NE])
        chosen = sb("chosen", [P, TT, NE])
        chosen_bf = sb("chosen_bf", [P, TT, NE], BF16)
        coef = sb("coef", [P, TT, NE])
        tok = sb("tok", [P, 5, TT])
        coefT = sb("coefT", [NE, TT * P])
        y_out = sb("y_out", [P, TT, E])

        q_scratch = nc.dram_tensor("q_scratch", (P, S), F32, kind="Internal").ap()

        bank = stack.enter_context(nc.psum_tensor("bank", [P, 8, 512], F32))

        ld_x, ld_a, ld_b = sem("ld_x"), sem("ld_a"), sem("ld_b")
        ld_pair = [sem("ld_pair0"), sem("ld_pair1")]
        sc_w, sc_r = sem("scratch_written"), sem("q_rep_loaded")
        g_const, v_set, pe_set, a_set = sem("g_const"), sem("v_set"), sem("pe_set"), sem("a_set")
        ld_toep = sem("toeplitz_loaded")
        pe_prep, v_prep, a_prep = sem("pe_prep"), sem("v_prep"), sem("a_prep")
        g_build = sem("g_build")
        pe_sa, v_maxa, a_expa, v_rca, g_na = sem("pe_scores_a"), sem("v_max_a"), sem("a_exp_a"), sem("v_recip_a"), sem("g_norm_a")
        pe_tra, v_eva, a_eva, pe_pva, v_oa = sem("pe_transposed_a"), sem("v_evac_a"), sem("a_evac_a"), sem("pe_pv_a"), sem("v_out_a")
        pe_wo, v_za, v_zb, v_ln, g_pow = sem("pe_wo"), sem("v_resid_a"), sem("v_resid_b"), sem("v_ln"), sem("g_pow")
        pe_xn, a_xn = sem("pe_xn"), sem("a_xn")
        pe_pj, a_pj, v_pj = sem("pe_proj"), sem("a_proj"), sem("v_proj")
        pe_sb, v_maxb, a_expb, v_rcb, g_nb = sem("pe_scores_b"), sem("v_max_b"), sem("a_exp_b"), sem("v_recip_b"), sem("g_norm_b")
        pe_trb, v_evb, v_evm, a_evb, pe_pvb, a_ob = sem("pe_transposed_b"), sem("v_evac_b"), sem("v_evac_mem"), sem("a_evac_b"), sem("pe_pv_b"), sem("a_out_b")
        pe_wob = sem("pe_wo_b")
        pe_m, v_m, a_m = sem("pe_moe"), sem("v_moe"), sem("a_moe")
        pe_y, v_gate, v_acc, v_lnf = sem("pe_expert"), sem("v_gate"), sem("v_acc"), sem("v_ln_final")
        g_powf, st_out = sem("g_pow_final"), sem("stored")

        x_rows = x.rearrange("b (t p) e -> b p t e", p=P)
        out_rows = out.rearrange("b (t p) e -> p (b t) e", p=P)

        passed = {name: sem(f"passed_{name}") for name in ("sp", "pool", "pe", "dve")}

        def stand_alone(eng, name):
            eng.sem_inc(passed[name])

        block = stack.enter_context(nc.Block())

        @block.sync
        def _(sp):
            for k, w in enumerate((wq, wk, wv)):
                sp.dma_start(wqkv[:, k, :], w).then_inc(ld_a, 16)
            sp.dma_start(bcols[:, 0:1], bq.rearrange("(p a) -> p a", a=1)).then_inc(ld_a, 16)
            sp.dma_start(bcols[:, 1:2], bk.rearrange("(p a) -> p a", a=1)).then_inc(ld_a, 16)
            sp.dma_start(rows[:, 0, :], bv.rearrange("(a n) -> a n", a=1)).then_inc(ld_a, 16)
            sp.dma_start(rows[:, 1, :], bo.rearrange("(a n) -> a n", a=1)).then_inc(ld_a, 16)
            sp.dma_start(rel_sb[:], rel.rearrange("(c p) d -> p c d", p=P)).then_inc(ld_a, 16)
            sp.sem_inc(sc_r, 16)
            with sp.Fori(0, NB) as b:
                sp.wait_ge(v_za, b + 1)
                stand_alone(sp, "sp")
                sp.dma_start(x_sb[:], x_rows[bass.ds(b, 1)].rearrange("b p t e -> (b p) t e")).then_inc(ld_x, 16)
                sp.wait_ge(sc_r, 16 * QI * b + 16)
                stand_alone(sp, "sp")
                sp.wait_ge(a_prep, b + 1)
                sp.dma_start(q_scratch, qT[:]).then_inc(sc_w, 16)
                sp.wait_ge(sc_w, 16 * b + 16)
                for i in range(QI):
                    sp.dma_start(q_rep[HD * i:HD * (i + 1), :, :],
                                 q_scratch.rearrange("(h d) i -> d h i", d=HD)).then_inc(sc_r, 16)

                def load_pair(p, k):
                    for j, src in enumerate((xwq[:, bass.ds(p * P, P)], xwkv[:, bass.ds(p * P, P)],
                                             xwkv[:, bass.ds(p * P + NP * P, P)], xwm[:, bass.ds(p * P, P)])):
                        sp.dma_start(w_pair[k][:, j, :], src).then_inc(ld_pair[k], 16)

                sp.wait_ge(pe_pj, 4 * NP * b + 1)
                load_pair(0, 0)
                load_pair(1, 1)
                with sp.Fori(1, NP // 2) as r:
                    for k in range(2):
                        sp.wait_ge(pe_pj, b * 4 * NP + r * 8 + (4 * k - 3))
                        load_pair(r * 2 + k, k)
            for n in range(TT // 4):
                sp.wait_ge(v_lnf, 2 * TT + 1 + 4 * (n + 1))
                sp.dma_start(out_rows[:, 4 * n:4 * n + 4, :], y_out[:, 4 * n:4 * n + 4, :]).then_inc(st_out, 16)
            sp.wait_ge(st_out, 16 * (TT // 4))

        @block.gpsimd
        def _(pool):
            def masked(out, base, mult, pattern, op, fill, n):
                pool.wait_ge(g_const, n)
                pool.affine_select(out=out, in_=out, compare_op=op, fill=fill, base=base, pattern=pattern,
                                   channel_multiplier=mult).then_inc(g_const, 1)

            pool.memset(ident[:], 0.0).then_inc(g_const, 1)
            masked(ident[:], 0, 1, [[-1, P]], ALU.not_equal, 1.0, 1)
            pool.memset(head_mask[:], 1.0).then_inc(g_const, 1)
            masked(head_mask[:], 0, 1, [[-HD, H]], ALU.is_ge, 0.0, 3)
            masked(head_mask[:], HD - 1, -1, [[HD, H]], ALU.is_ge, 0.0, 4)
            pool.memset(toep[:], 0.0).then_inc(g_const, 1)
            masked(toep[:], WIN - QI * HD, 1, [[-1, TW]], ALU.is_ge, NEG, 6)
            for k in range(2):
                pool.memset(q_pos[k][:], 0.0).then_inc(g_const, 1)
            pool.memset(ones_row[:], 1.0).then_inc(g_const, 1)
            for k in range(2):
                masked(q_pos[k][:].rearrange("p (t i) h -> p t i h", i=QI), -QI * HD, 1,
                       [[0, GT], [-1, QI], [0, H]], ALU.not_equal, 1.0, 9)
            pool.memset(power[:], -0.5).then_inc(g_const, 1)
            pool.memset(ones_bf[:], 1.0).then_inc(g_const, 1)
            pool.memset(before[:], 1.0).then_inc(g_const, 1)
            masked(before[:], -1, -1, [[1, P]], ALU.is_ge, 0.0, 15)
            pool.iota(rank[:], [[-1, NE]], base=NE, channel_multiplier=0, allow_small_or_imprecise_dtypes=True).then_inc(g_const, 1)

            with pool.Fori(0, NB) as b:
                def build(g):
                    k = g % 2
                    if g == 0:
                        pool.wait_ge(a_prep, b + 1)
                    if g >= 2:
                        pool.wait_ge(pe_sa, b * (G * GT) + GT * (g - 1))
                    cols = qT[:, GI * g:GI * (g + 1)].unsqueeze(2).broadcast_to([P, GI, H])
                    pool.tensor_tensor(q_heads[k][:], cols, head_mask[:].unsqueeze(1).broadcast_to([P, GI, H]),
                                       ALU.mult).then_inc(g_build, 1)
                    if g == 0:
                        pool.wait_ge(sc_r, 16 * QI * b + 16 * (QI + 1))
                    n = QI * HD
                    rep = q_rep[:, :, GI * g:GI * (g + 1)].rearrange("p h (t i) -> p t i h", i=QI)
                    pick = head_mask[0:n, 0:QI].unsqueeze(1).unsqueeze(3).broadcast_to([n, GT, QI, H])
                    pool.tensor_tensor(q_pos[k][0:n].rearrange("p (t i) h -> p t i h", i=QI), rep, pick,
                                       ALU.mult).then_inc(g_build, 1)

                build(0)
                build(1)
                for g in range(G):
                    n = GI * (g + 1)
                    for t in range(GT):
                        pool.wait_ge(v_rca, b * (G * GT) + GT * g + t + 1)
                        stand_alone(pool, "pool")
                        row = prob_a[g % 2][:, t, 0:n]
                        pool.tensor_scalar(row, row, stat_a[:, 2, g % 2, t:t + 1], 1.0, ALU.mult,
                                           ALU.mult).then_inc(g_na, 1)
                    if g + 2 < G:
                        build(g + 2)

                def rsqrt(n):
                    pool.wait_ge(v_ln, b * (3 * LN) + LN * n + 2 * T + 1)
                    pool.tensor_tensor(rstd[:, 0:T], var_eps[:, 0:T], power[:, 0:T], ALU.pow).then_inc(g_pow, 1)

                rsqrt(0)
                rsqrt(1)

                def normalise(u):
                    for h in range(2):
                        pool.wait_ge(v_rcb, u * 2 + (h + 1))
                        stand_alone(pool, "pool")
                        pool.tensor_scalar(prob_b[h][:], prob_b[h][:], stat_b[:, 2, h:h + 1], 1.0, ALU.mult,
                                           ALU.mult).then_inc(g_nb, 1)

                with pool.Fori(0, NU) as u:
                    normalise(b * NU + u)
                rsqrt(2)
            pool.wait_ge(v_lnf, 2 * TT + 1)
            pool.tensor_tensor(rstd[:], var_eps[:], power[:], ALU.pow).then_inc(g_powf, 1)

        @block.scalar
        def _(act):
            def copy(out, in_, done):
                act.activation(out, in_, ACT.Copy).then_inc(done, 1)

            act.dma_start(wo_sb[:], wo).then_inc(ld_b, 16)
            act.dma_start(xwo_sb[:], xwo.rearrange("(c p) n -> p c n", p=P)).then_inc(ld_b, 16)
            act.dma_start(rows[:, 2, :], xbo.rearrange("(a n) -> a n", a=1)).then_inc(ld_b, 16)
            act.dma_start(bcols[:, 2:3], ln_g.rearrange("(p a) -> p a", a=1)).then_inc(ld_b, 16)
            act.dma_start(bcols[:, 3:4], ln_b.rearrange("(p a) -> p a", a=1)).then_inc(ld_b, 16)
            act.dma_start(ctx_sb[:], ctx.rearrange("b m e -> (b m) e")).then_inc(ld_b, 16)
            act.dma_start(wg_sb[:], wg).then_inc(ld_b, 16)
            act.dma_start(we_sb[:], we.rearrange("e f h -> f e h")).then_inc(ld_b, 16)
            act.dma_start(be_sb[:], be).then_inc(ld_b, 16)

            act.wait_ge(pe_set, 1)
            r_cols = bank[0:HD, 0, 0:REL]
            copy(rel_ext[:, REL:2 * REL], r_cols, a_set)
            act.activation(rel_ext[:, 0:REL], r_cols[:, 0:1].broadcast_to([HD, REL]), ACT.Copy).then_inc(a_set, 1)
            rest = TW + QI - 2 * REL
            act.activation(rel_ext[:, 2 * REL:], r_cols[:, REL - 1:REL].broadcast_to([HD, rest]), ACT.Copy).then_inc(a_set, 1)
            act.wait_ge(a_set, 3)
            act.wait_ge(g_const, 10)
            for i in range(QI):
                act.dma_start(toep[HD * i:HD * (i + 1), :],
                             rel_ext[:, QI - 1 - i:QI - 1 - i + TW]).then_inc(ld_toep, 16)
            act.wait_ge(pe_set, 4)
            copy(weT[:, 0:4, :], bank[:, 1, :].rearrange("p (e f) -> p e f", f=E), a_set)
            copy(weT[:, 4:8, :], bank[:, 2, :].rearrange("p (e f) -> p e f", f=E), a_set)
            copy(ctxT[:], bank[:, 3, 0:NB * M], a_set)

            act.sem_inc(a_ob)
            with act.Fori(0, NB) as b:
                act.wait_ge(pe_prep, b * 4 + 2)
                act.wait_ge(v_set, 1)
                act.activation(qT[:], bank[:, 4, :], ACT.Identity, bias=bcols[:, 4:5],
                               scale=SCALE_A).then_inc(a_prep, 1)

                def exp_a(g, t):
                    act.wait_ge(v_maxa, b * (G * GT) + GT * g + t + 1)
                    n = GI * (g + 1)
                    act.activation(prob_a[g % 2][:, t, 0:n], bank[:, t, 0:n], ACT.Exp,
                                   bias=stat_a[:, 0, g % 2, t:t + 1], scale=1.0,
                                   accum_out=stat_a[:, 1, g % 2, t:t + 1]).then_inc(a_expa, 1)

                for t in range(GT):
                    exp_a(0, t)
                for g in range(G):
                    for t in range(GT):
                        if g + 1 < G:
                            exp_a(g + 1, t)
                        n = TR0[g] + t
                        if t < chunks(g) and n % 2 == 1:
                            rows_n = min(P, GI * (g + 1) - P * t)
                            act.wait_ge(pe_tra, b * NTR + n + 1)
                            copy(probT_a[0:rows_n, t, :], bank[0:rows_n, 5, :], a_eva)

                act.wait_ge(pe_xn, b + 1)
                act.wait_ge(ld_b, 16 * N_LOADS_B)
                act.activation(xnT[:], bank[:, 7, :], ACT.Identity, bias=bcols[:, 3:4],
                               scale=bcols[:, 2:3]).then_inc(a_xn, 1)

                def piece(p, k, j):
                    if j == 3:
                        return
                    act.wait_ge(pe_pj, b * (4 * NP) + p * 4 + (j + 2))
                    if j == 0:
                        act.activation(q_pair[k][:], bank[:, 7, :], ACT.Copy, scale=SCALE_B).then_inc(a_pj, 1)
                    if j == 1:
                        copy(k_head[k][0][0:XD, 0:S], bank[0:XD, 7, :], a_pj)
                    if j == 2:
                        for h in range(2):
                            part = slice(XD * h, XD * (h + 1))
                            copy(k_head[k][h][part, S:KEYS], bank[part, 7, 0:M], a_pj)
                        copy(vm_pair[k][:], bank[0:M, 7, P:2 * P], a_pj)

                def exp_b(u, h):
                    act.wait_ge(v_maxb, u * 2 + (h + 1))
                    act.activation(prob_b[h][:].rearrange("p (c n) -> p c n", c=2), bank[:, 2 * h:2 * h + 2, 0:KH],
                                   ACT.Exp, bias=stat_b[:, 0, h:h + 1], scale=1.0,
                                   accum_out=stat_b[:, 1, h:h + 1]).then_inc(a_expb, 1)

                def unit(p, k, it, last_pair):
                    u = b * NU + p * 4 + it
                    last = last_pair and it == T - 1
                    if not last_pair:
                        piece(p + 1, 1 - k, it)
                    if not last:
                        exp_b(u + 1, 0)
                    act.wait_ge(pe_trb, u * 2 + 2)
                    copy(probT_b[1][:], bank[:, 5, :].rearrange("p (c n) -> p c n", n=P), a_evb)
                    if not last:
                        exp_b(u + 1, 1)
                    act.wait_ge(pe_pvb, u + 1)
                    copy(outT_b[:, bass.ds(p, 1), it * P:(it + 1) * P], bank[:, 6, 0:P].unsqueeze(1), a_ob)

                for j in range(4):
                    piece(0, 0, j)
                for h in range(2):
                    exp_b(b * NU, h)
                with act.Fori(0, NP // 2 - 1) as r:
                    for k in range(2):
                        for it in range(T):
                            unit(r * 2 + k, k, it, False)
                for k in range(2):
                    for it in range(T):
                        unit(NP - 2 + k, k, it, k == 1)

            act.wait_ge(pe_m, 1)
            copy(x2T[:, 512:1024], bank[:, 1, :], a_m)
            act.wait_ge(v_m, 3)
            act.activation(ex[:], lg[:], ACT.Exp).then_inc(a_m, 1)
            act.wait_ge(pe_m, 4)
            copy(coefT[:, 512:1024], bank[0:NE, 5, :], a_m)

        @block.tensor
        def _(pe):
            def transpose_to(out, in_, k=P):
                return pe.transpose(out, in_, ident[0:k, 0:k])

            def add_bias(n, row):
                return pe.matmul(bank[:, n, :], ones_row[:], rows[:, row, :].unsqueeze(1).broadcast_to([1, T, E]),
                                 start=False, stop=True, skip_group_check=True)

            pe.wait_ge(ld_a, 16 * N_LOADS_A)
            pe.wait_ge(g_const, 10)
            for c in range(REL // P):
                last = transpose_to(bank[0:HD, 0, c * P:(c + 1) * P], rel_sb[:, c, :])
            last.then_inc(pe_set, 1)

            def setup_rest():
                pe.wait_ge(ld_b, 16 * N_LOADS_B)
                for c in range(2):
                    for e in range(4):
                        last = transpose_to(bank[:, 1 + c, e * E:(e + 1) * E], we_sb[:, 4 * c + e, :])
                    last.then_inc(pe_set, 1)
                transpose_to(bank[:, 3, 0:NB * M], ctx_sb[:], NB * M).then_inc(pe_set, 1)

            setup_rest()
            pe.wait_ge(v_set, 6)
            pe.wait_ge(a_set, 6)

            pe.sem_inc(pe_pj)
            with pe.Fori(0, NB) as b:
                pe.wait_ge(ld_x, 16 * b + 16)
                for t in range(T):
                    last = transpose_to(bank[:, 7, t * P:(t + 1) * P], x_sb[:, t, :])
                last.then_inc(pe_prep, 1)
                pe.wait_ge(v_prep, b * 4 + 1)
                pe.wait_ge(a_ob, b * NU + 1)
                pe.wait_ge(v_zb, b + 1)
                pe.matmul(bank[:, 4, :], wqkv[:, 0, :], xT[:], start=True, stop=True).then_inc(pe_prep, 1)
                pe.matmul(bank[:, 5, :], wqkv[:, 1, :], xT[:], start=True, stop=True).then_inc(pe_prep, 1)
                for t in range(T):
                    pe.matmul(bank[:, 6, t * E:(t + 1) * E], xT[:, t * P:(t + 1) * P], wqkv[:, 2, :],
                              start=(t == 0), stop=False, skip_group_check=True)
                add_bias(6, 0).then_inc(pe_prep, 1)

                def scores_a(g, t):
                    if t == 0:
                        pe.wait_ge(g_build, b * (2 * G) + 2 * (g + 1))
                    if g == 0 and t == 0:
                        pe.wait_ge(v_prep, b * 4 + 2)
                        pe.wait_ge(ld_toep, 16 * QI)
                    if g > 0:
                        pe.wait_ge(a_expa, b * (G * GT) + GT * (g - 1) + t + 1)
                    n = GI * (g + 1)
                    first = WIN - (GI * g + QI * t)
                    tile = slice(QI * t, QI * (t + 1))
                    pe.matmul(bank[:, t, 0:n], q_heads[g % 2][:, tile, :], kT[:, 0:n], start=True, stop=False)
                    pe.matmul(bank[:, t, 0:n], q_pos[g % 2][:, tile, :], toep[:, first:first + n],
                              start=False, stop=True).then_inc(pe_sa, 1)

                def evacuated(n):
                    done, per = ((v_eva, a_eva)[n % 2], NTR // 2)
                    pe.wait_ge(done, b * per + n // 2 + 1)

                def transposes_a(g, c):
                    n = TR0[g] + c
                    if c == 0:
                        pe.wait_ge(g_na, b * (G * GT) + GT * (g + 1))
                    if g == 0 and c == 0:
                        pe.wait_ge(a_prep, b + 1)
                        pe.wait_ge(v_prep, b * 4 + 3)
                    if n >= 2:
                        evacuated(n - 2)
                    rows_n = min(P, GI * (g + 1) - P * c)
                    stand_alone(pe, "pe")
                    for t in range(GT):
                        last = transpose_to(bank[0:rows_n, 4 + n % 2, t * P:(t + 1) * P],
                                            prob_a[g % 2][:, t, c * P:c * P + rows_n])
                    last.then_inc(pe_tra, 1)

                def pv_a(g, c):
                    evacuated(TR0[g] + c)
                    if c == 0 and g > 0:
                        pe.wait_ge(v_oa, b * (2 * G) + 2 * (g - 1) + 1)
                    rows_n = min(P, GI * (g + 1) - P * c)
                    stand_alone(pe, "pe")
                    for q in range(4):
                        moving = probT_a[0:rows_n, c, :].rearrange("p (i h) -> p i h", h=H)[:, :, 4 * q:4 * q + 4]
                        last = pe.matmul(bank[32 * q:32 * q + 32, 6, 0:P], v_sb[0:rows_n, c, 32 * q:32 * q + 32],
                                         moving, start=(c == 0), stop=(c == chunks(g) - 1),
                                         tile_position=(0, 32 * q))
                    if c == chunks(g) - 1:
                        last.then_inc(pe_pva, 1)

                for t in range(GT):
                    scores_a(0, t)
                for g in range(G):
                    for t in range(GT):
                        if g + 1 < G:
                            scores_a(g + 1, t)
                        if t < chunks(g):
                            transposes_a(g, t)
                        if 1 <= t <= chunks(g):
                            pv_a(g, t - 1)
                    if chunks(g) == GT:
                        pv_a(g, GT - 1)

                pe.wait_ge(v_oa, b * (2 * G) + 2 * G)
                for t in range(T):
                    pe.matmul(bank[:, 5, t * E:(t + 1) * E], outT_a[:, t * P:(t + 1) * P], wo_sb[:],
                              start=(t == 0), stop=False, skip_group_check=True)
                add_bias(5, 1).then_inc(pe_wo, 1)

                pe.wait_ge(v_ln, b * (3 * LN) + 2 * LN)
                for t in range(T):
                    last = transpose_to(bank[:, 7, t * P:(t + 1) * P], x1n[:, t, :])
                last.then_inc(pe_xn, 1)

                def piece(p, k, j):
                    a_n, v_n = b * (5 * NP) + p * 5, b * (2 * NP) + p * 2 + 1
                    if j == 0:
                        pe.wait_ge(v_pj, v_n)
                        pe.wait_ge(ld_pair[k], b * (64 * NP // 2) + (p + (2 - k)) * 32)
                        pe.matmul(bank[:, 7, :], w_pair[k][:, 0, :], xnT[:], start=True, stop=True).then_inc(pe_pj, 1)
                    if j == 1:
                        pe.wait_ge(a_pj, a_n + 1)
                        pe.matmul(bank[:, 7, :], w_pair[k][:, 1, :], xnT[:], start=True, stop=True).then_inc(pe_pj, 1)
                    if j == 2:
                        pe.wait_ge(a_pj, a_n + 2)
                        pe.wait_ge(v_pj, v_n + 1)
                        pe.matmul(bank[:, 7, 0:M], w_pair[k][:, 3, :], ctxT_b[:], start=True, stop=True)
                        pe.matmul(bank[0:M, 7, P:2 * P], ctxT_b[:], w_pair[k][:, 3, :], start=True,
                                  stop=True).then_inc(pe_pj, 1)
                    if j == 3:
                        pe.wait_ge(a_pj, a_n + 5)
                        for t in range(T):
                            last = pe.matmul(bank[:, 7, t * P:(t + 1) * P], xnT[:, t * P:(t + 1) * P],
                                             w_pair[k][:, 2, :], start=True, stop=True)
                        last.then_inc(pe_pj, 1)

                def scores_b(p, k, it, h):
                    if it == 0 and h == 0:
                        pe.wait_ge(a_pj, b * (5 * NP) + p * 5 + 5)
                        pe.wait_ge(v_pj, b * (2 * NP) + p * 2 + 2)
                    for c in range(2):
                        last = pe.matmul(bank[:, 2 * h + c, 0:KH], q_pair[k][:, it * P:(it + 1) * P],
                                         k_head[k][h][:, c * KH:(c + 1) * KH], start=True, stop=True)
                    last.then_inc(pe_sb, 1)

                def unit(p, k, it, last_pair):
                    u = b * NU + p * 4 + it
                    if not last_pair:
                        piece(p + 1, 1 - k, it)
                    for h in range(2):
                        pe.wait_ge(g_nb, u * 2 + (h + 1))
                        if h == 0:
                            pe.wait_ge(a_ob, u + 1)
                        stand_alone(pe, "pe")
                        for c in range(T):
                            transpose_to(bank[:, 4 + h, c * P:(c + 1) * P], prob_b[h][:, c * P:(c + 1) * P])
                        transpose_to(bank[0:M, 6, h * P:(h + 1) * P], prob_b[h][:, S:KEYS]).then_inc(pe_trb, 1)
                        if it < T - 1:
                            scores_b(p, k, it + 1, h)
                        elif not last_pair:
                            scores_b(p + 1, 1 - k, 0, h)
                    pe.wait_ge(v_evb, u + 1)
                    pe.wait_ge(v_evm, u + 1)
                    pe.wait_ge(a_evb, u + 1)
                    if it == 0:
                        pe.wait_ge(v_pj, b * (2 * NP) + p * 2 + 3)
                    for c in range(T + 1):
                        for h in range(2):
                            half = slice(XD * h, XD * (h + 1))
                            if c < T:
                                vals, probs = v_pair[k][:, c, half], probT_b[h][:, c, :]
                            else:
                                vals, probs = vm_pair[k][:, half], probTm[:, h, :]
                            last = pe.matmul(bank[half, 6, 0:P], vals, probs, start=(c == 0), stop=(c == T),
                                             tile_position=(0, XD * h))
                    last.then_inc(pe_pvb, 1)

                pe.wait_ge(a_xn, b + 1)
                pe.wait_ge(v_prep, b * 4 + 4)
                for j in range(4):
                    piece(0, 0, j)
                for h in range(2):
                    scores_b(0, 0, 0, h)
                with pe.Fori(0, NP // 2 - 1) as r:
                    for k in range(2):
                        for it in range(T):
                            unit(r * 2 + k, k, it, False)
                for k in range(2):
                    for it in range(T):
                        unit(NP - 2 + k, k, it, k == 1)

                pe.wait_ge(a_ob, b * NU + (NU + 1))
                for p in range(NP):
                    for t in range(T):
                        pe.matmul(bank[:, 4, t * E:(t + 1) * E], outT_b[:, p, t * P:(t + 1) * P],
                                  xwo_sb[:, p, :], start=(p == 0 and t == 0), stop=False, skip_group_check=True)
                add_bias(4, 2).then_inc(pe_wob, 1)

            pe.wait_ge(v_ln, NB * 3 * LN)
            for t in range(TT):
                last = transpose_to(bank[:, t // 4, (t % 4) * P:(t % 4 + 1) * P], x2[:, t, :])
            last.then_inc(pe_m, 1)
            pe.wait_ge(v_m, 1)
            pe.wait_ge(a_m, 1)
            for t in range(TT):
                last = pe.matmul(bank[:, 2, t * NE:(t + 1) * NE], x2T[:, t * P:(t + 1) * P], wg_sb[:],
                                 start=True, stop=True)
            last.then_inc(pe_m, 1)
            pe.wait_ge(v_m, 9)
            pe.wait_ge(g_const, 17)
            for t in range(TT - 1):
                pe.matmul(bank[:, 3, (t + 1) * NE:TT * NE], ones_bf[:],
                          chosen_bf[:, t:t + 1, :].broadcast_to([P, TT - 1 - t, NE]),
                          start=(t == 0), stop=False, skip_group_check=True)
            pe.matmul(bank[:, 3, 0:TT * NE], before[:], chosen_bf[:].rearrange("p t e -> p (t e)"),
                      start=False, stop=True, skip_group_check=True).then_inc(pe_m, 1)
            pe.wait_ge(v_m, 11)
            pe.wait_ge(v_zb, NB + 1)
            for t in range(TT):
                last = transpose_to(bank[0:NE, 4 + t // 4, (t % 4) * P:(t % 4 + 1) * P], coef[:, t, :])
            last.then_inc(pe_m, 1)
            pe.wait_ge(v_m, 12)
            pe.wait_ge(a_m, 3)
            for t in range(TT):
                if t >= 3:
                    pe.wait_ge(v_acc, (NE + 1) * (t - 2))
                for c in range(2):
                    pe.matmul(bank[:, EXPERT_BANKS[t % 3] + c, :], x2T[:, t * P:(t + 1) * P],
                              weT[:, 4 * c:4 * c + 4, :].rearrange("p e f -> p (e f)"), start=True, stop=True)
                if t >= 2:
                    pe.wait_ge(v_acc, (NE + 1) * (t - 1))
                pe.matmul(bank[:, 4 + t % 2, 0:E], coefT[:, t * P:(t + 1) * P], be_sb[:], start=True,
                          stop=True).then_inc(pe_y, 1)

        @block.vector
        def _(dve):
            dve.wait_ge(ld_a, 16 * N_LOADS_A)
            dve.tensor_scalar(bcols[:, 4:5], bcols[:, 0:1], SCALE_A, None, ALU.mult).then_inc(v_set, 1)
            dve.wait_ge(g_const, 5)
            dve.tensor_reduce(quad_mask[:], head_mask[:].rearrange("p (c q) -> p q c", q=4), AX.X,
                              ALU.add).then_inc(v_set, 1)
            for k in range(2):
                dve.memset(k_head[k][0][XD:, :], 0.0).then_inc(v_set, 1)
                dve.memset(k_head[k][1][0:XD, :], 0.0).then_inc(v_set, 1)
            dve.wait_ge(v_set, 6)

            for free in (v_za, v_zb, v_pj):
                dve.sem_inc(free)

            with dve.Fori(0, NB) as b:
                n_ln = b * (3 * LN)

                dve.wait_ge(pe_prep, b * 4 + 1)
                dve.tensor_copy(xT[:], bank[:, 7, :]).then_inc(v_prep, 1)
                dve.wait_ge(pe_prep, b * 4 + 3)
                dve.tensor_scalar(kT[:], bank[:, 5, :], bcols[:, 1:2], None, ALU.add).then_inc(v_prep, 1)
                dve.wait_ge(pe_prep, b * 4 + 4)
                dve.tensor_copy(v_sb[:], bank[:, 6, :].rearrange("p (t e) -> p t e", e=E)).then_inc(v_prep, 1)

                def max_a(g, t):
                    dve.wait_ge(pe_sa, b * (G * GT) + GT * g + t + 1)
                    dve.tensor_reduce(stat_a[:, 0, g % 2, t:t + 1], bank[:, t, 0:GI * (g + 1)], AX.X, ALU.max,
                                      negate=True).then_inc(v_maxa, 1)

                def recip_a(g, t):
                    dve.wait_ge(a_expa, b * (G * GT) + GT * g + t + 1)
                    dve.reciprocal(stat_a[:, 2, g % 2, t:t + 1], stat_a[:, 1, g % 2, t:t + 1]).then_inc(v_rca, 1)

                for t in range(GT):
                    max_a(0, t)
                for t in range(GT):
                    recip_a(0, t)
                for g in range(G):
                    for t in range(GT):
                        if g + 1 < G:
                            max_a(g + 1, t)
                            if t > 0:
                                recip_a(g + 1, t - 1)
                        n = TR0[g] + t
                        if t < chunks(g) and n % 2 == 0:
                            rows_n = min(P, GI * (g + 1) - P * t)
                            dve.wait_ge(pe_tra, b * NTR + n + 1)
                            dve.tensor_copy(probT_a[0:rows_n, t, :], bank[0:rows_n, 4, :]).then_inc(v_eva, 1)
                    if g + 1 < G:
                        recip_a(g + 1, GT - 1)
                    dve.wait_ge(pe_pva, b * G + g + 1)
                    dve.tensor_tensor(o_masked[:], bank[:, 6, 0:P].rearrange("p (i q) -> p i q", q=4),
                                      quad_mask[:].unsqueeze(1).broadcast_to([P, GI, 4]), ALU.mult).then_inc(v_oa, 1)
                    dve.wait_ge(v_oa, b * (2 * G) + 2 * g + 1)
                    dve.tensor_reduce(outT_a[:, GI * g:GI * (g + 1)], o_masked[:], AX.X, ALU.add).then_inc(v_oa, 1)

                def layernorm(src, n, write):
                    v0 = n_ln + LN * n
                    for t in range(T):
                        dve.bn_stats(stats[:, t, :], src[:, t, :]).then_inc(v_ln, 1)
                    for t in range(T):
                        dve.wait_ge(v_ln, v0 + t + 1)
                        stand_alone(dve, "dve")
                        dve.bn_aggr(moments[:, t, :], stats[:, t, :]).then_inc(v_ln, 1)
                    dve.wait_ge(v_ln, v0 + 2 * T)
                    dve.tensor_scalar(var_eps[:, 0:T], moments[:, 0:T, 1], EPS, None, ALU.add).then_inc(v_ln, 1)
                    dve.wait_ge(g_pow, b * 3 + n + 1)
                    for t in range(T):
                        dve.tensor_scalar(write(t), src[:, t, :], moments[:, t, 0:1], rstd[:, t:t + 1],
                                          ALU.subtract, ALU.mult).then_inc(v_ln, 1)
                    dve.wait_ge(v_ln, v0 + 3 * T + 1)

                dve.wait_ge(pe_wo, b + 1)
                dve.tensor_tensor(z[:, 0:T, :], bank[:, 5, :].rearrange("p (t e) -> p t e", e=E), x_sb[:],
                                  ALU.add).then_inc(v_za, 1)
                dve.wait_ge(v_za, b + 2)
                layernorm(z, 0, lambda t: x1[:, t, :])
                dve.wait_ge(a_set, 6)
                dve.tensor_copy(ctxT_b[:], ctxT[:, bass.ds(b * M, M)]).then_inc(v_prep, 1)
                layernorm(x1, 1, lambda t: x1n[:, t, :])

                def piece(p, k, j):
                    if j == 1:
                        dve.wait_ge(pe_pj, b * (4 * NP) + p * 4 + 3)
                        dve.tensor_copy(k_head[k][1][XD:P, 0:S], bank[XD:P, 7, :]).then_inc(v_pj, 1)
                    if j == 3:
                        dve.wait_ge(pe_pj, b * (4 * NP) + p * 4 + 5)
                        dve.tensor_copy(v_pair[k][:], bank[:, 7, :].rearrange("p (t n) -> p t n", n=P)).then_inc(v_pj, 1)

                def max_b(u, h):
                    dve.wait_ge(pe_sb, u * 2 + (h + 1))
                    dve.tensor_reduce(stat_b[:, 0, h:h + 1], bank[:, 2 * h:2 * h + 2, 0:KH], AX.XY, ALU.max,
                                      negate=True).then_inc(v_maxb, 1)

                def recips_b(u):
                    for h in range(2):
                        dve.wait_ge(a_expb, u * 2 + (h + 1))
                        dve.reciprocal(stat_b[:, 2, h:h + 1], stat_b[:, 1, h:h + 1]).then_inc(v_rcb, 1)

                def unit(p, k, it, last_pair):
                    u = b * NU + p * 4 + it
                    last = last_pair and it == T - 1
                    if not last_pair:
                        piece(p + 1, 1 - k, it)
                    dve.wait_ge(pe_trb, u * 2 + 1)
                    dve.tensor_copy(probT_b[0][:], bank[:, 4, :].rearrange("p (c n) -> p c n", n=P)).then_inc(v_evb, 1)
                    if not last:
                        max_b(u + 1, 0)
                    dve.wait_ge(pe_trb, u * 2 + 2)
                    dve.tensor_copy(probTm[:], bank[0:M, 6, 0:2 * P].rearrange("p (h n) -> p h n", n=P)).then_inc(v_evm, 1)
                    if not last:
                        max_b(u + 1, 1)
                        recips_b(u + 1)

                for j in range(4):
                    piece(0, 0, j)
                for h in range(2):
                    max_b(b * NU, h)
                recips_b(b * NU)
                with dve.Fori(0, NP // 2 - 1) as r:
                    for k in range(2):
                        for it in range(T):
                            unit(r * 2 + k, k, it, False)
                for k in range(2):
                    for it in range(T):
                        unit(NP - 2 + k, k, it, k == 1)

                dve.wait_ge(pe_wob, b + 1)
                dve.tensor_tensor(z[:, 0:T, :], bank[:, 4, :].rearrange("p (t e) -> p t e", e=E), x1[:],
                                  ALU.add).then_inc(v_zb, 1)
                dve.wait_ge(v_zb, b + 2)
                layernorm(z, 2, lambda t: x2[:, bass.ds(b * T + t, 1), :])

            def step(ins, n):
                ins.then_inc(v_m, 1)
                dve.wait_ge(v_m, n)

            def over_experts(col):
                return tok[:, col, :].unsqueeze(2).broadcast_to([P, TT, NE])

            dve.wait_ge(pe_m, 1)
            step(dve.tensor_copy(x2T[:, 0:512], bank[:, 0, :]), 1)
            dve.wait_ge(pe_m, 2)
            logits = bank[:, 2, 0:TT * NE].rearrange("p (t e) -> p t e", e=NE)
            step(dve.tensor_reduce(tok[:, 0, :], logits, AX.X, ALU.max), 2)
            step(dve.tensor_tensor(lg[:], logits, over_experts(0), ALU.subtract), 3)
            dve.wait_ge(a_m, 2)
            step(dve.tensor_reduce(tok[:, 1, :], ex[:], AX.X, ALU.max), 4)
            step(dve.tensor_tensor(cand[:], ex[:], over_experts(1), ALU.is_ge), 5)
            dve.wait_ge(g_const, 17)
            step(dve.tensor_tensor(cand[:], cand[:], rank[:].unsqueeze(1).broadcast_to([P, TT, NE]), ALU.mult), 6)
            step(dve.tensor_reduce(tok[:, 4, :], cand[:], AX.X, ALU.max), 7)
            step(dve.tensor_tensor(chosen[:], cand[:], over_experts(4), ALU.is_equal), 8)
            step(dve.tensor_copy(chosen_bf[:], chosen[:]), 9)
            dve.tensor_reduce(tok[:, 2, :], ex[:], AX.X, ALU.add).then_inc(v_gate, 1)
            dve.wait_ge(v_gate, 1)
            dve.reciprocal(tok[:, 2, :], tok[:, 2, :]).then_inc(v_gate, 1)
            dve.wait_ge(v_gate, 2)
            dve.tensor_tensor(tok[:, 3, :], tok[:, 1, :], tok[:, 2, :], ALU.mult).then_inc(v_gate, 1)
            dve.wait_ge(v_gate, 3)
            dve.wait_ge(pe_m, 3)
            places = bank[:, 3, 0:TT * NE].rearrange("p (t e) -> p t e", e=NE)
            step(dve.scalar_tensor_tensor(out=coef[:], in0=places, scalar=float(CAP), in1=chosen[:],
                                          op0=ALU.is_lt, op1=ALU.mult), 10)
            step(dve.tensor_tensor(coef[:], coef[:], over_experts(3), ALU.mult), 11)
            dve.wait_ge(pe_m, 4)
            step(dve.tensor_copy(coefT[:, 0:512], bank[0:NE, 4, :]), 12)
            for t in range(TT):
                dve.wait_ge(pe_y, t + 1)
                for e in range(NE):
                    y = bank[:, EXPERT_BANKS[t % 3] + e // 4, (e % 4) * E:(e % 4 + 1) * E]
                    if e:
                        dve.wait_ge(v_acc, (NE + 1) * t + e)
                    dve.scalar_tensor_tensor(out=z[:, t, :], in0=y, scalar=coef[:, t, e:e + 1],
                                             in1=(z if e else x2)[:, t, :], op0=ALU.mult,
                                             op1=ALU.add).then_inc(v_acc, 1)
                dve.wait_ge(v_acc, (NE + 1) * t + NE)
                dve.tensor_tensor(z[:, t, :], bank[:, 4 + t % 2, 0:E], z[:, t, :], ALU.add).then_inc(v_acc, 1)
                dve.wait_ge(v_acc, (NE + 1) * (t + 1))
                dve.bn_stats(stats[:, t, :], z[:, t, :]).then_inc(v_lnf, 1)
            for t in range(TT):
                dve.wait_ge(v_lnf, t + 1)
                dve.bn_aggr(moments[:, t, :], stats[:, t, :]).then_inc(v_lnf, 1)
            dve.wait_ge(v_lnf, 2 * TT)
            dve.tensor_scalar(var_eps[:], moments[:, :, 1], EPS, None, ALU.add).then_inc(v_lnf, 1)
            dve.wait_ge(g_powf, 1)
            for t in range(TT):
                dve.tensor_scalar(y_out[:, t, :], z[:, t, :], moments[:, t, 0:1], rstd[:, t:t + 1],
                                  ALU.subtract, ALU.mult).then_inc(v_lnf, 1)


_INS = ['x', 'ctx_1024', 'L0_attn_Wq', 'L0_attn_bq', 'L0_attn_Wk', 'L0_attn_bk', 'L0_attn_Wv', 'L0_attn_bv',
        'L0_attn_Wo', 'L0_attn_bo', 'L0_attn_rel_key', 'L0_xattn_ln_g', 'L0_xattn_ln_b', 'L0_xattn_Wq',
        'L0_xattn_Wkv', 'L0_xattn_Wm', 'L0_xattn_Wo', 'L0_xattn_bo', 'L0_ffn_wg', 'L0_ffn_W', 'L0_ffn_b']


def kernel(**inputs):
    import numpy as np
    import concourse.bacc as bacc
    from concourse.bass_utils import run_bass_kernel_spmd

    nc = bacc.Bacc("TRN2", target_bir_lowering=False, num_devices=1)
    arrays, args = {}, []
    for name in _INS:
        a = np.ascontiguousarray(inputs[name])
        arrays[f"in_{name}"] = a
        args.append(nc.dram_tensor(f"in_{name}", a.shape, mybir.dt.from_np(a.dtype), kind="ExternalInput").ap())
    out = nc.dram_tensor("out_x", (NB, S, E), F32, kind="ExternalOutput").ap()
    decoder_layer(nc, *args, out)
    return run_bass_kernel_spmd(nc, [arrays], core_ids=[0]).results[0]["out_x"]
```

```python
from contextlib import ExitStack

import concourse.bass as bass
from concourse import mybir
from concourse.alu_op_type import AluOpType as ALU

F32 = mybir.dt.float32
F32R = mybir.dt.float32r
BF16 = mybir.dt.bfloat16
ACT = mybir.ActivationFunctionType
AX = mybir.AxisListType

P = 128
NB, S, E = 2, 512, 128
T = S // P
EPS = 1e-5
NEG = -1e30

H, HD, REL = 16, 8, 256
QI = P // H
GI = 32
GT = GI // QI
G = S // GI
WIN = S - QI
TW = WIN + GI
SCALE_A = HD ** -0.5


def chunks(g):
    return -(-GI * (g + 1) // P)


TR0 = [sum(chunks(k) for k in range(g)) for g in range(G + 1)]
NTR = TR0[G]
assert NTR % 4 == 0

XD, M = 64, 32
NP = 8
KEYS = S + M
KH = KEYS // 2
NU = NP * T
SCALE_B = XD ** -0.5

NE, CAP = 8, NB * S // 8
EXPERT_BANKS = (0, 2, 6)
TT = NB * T

PREP_1 = (1, 3, 5, 7)
SETUP = (9, 11, 13)
WO_0, LN_0, APPLY_0, LN_1, APPLY_1, XN_0 = 17, 18, 20, 21, 23, 24
PIECES_0 = (25, 26, 27, 28)
LNS = ((0, "attention"), (0, "inner"), (1, "attention"), (1, "inner"), (0, "memories"), (1, "memories"))
LN_MORE = 2 * T + 1
LN_BEGIN, LN = 2 * T + 1, 3 * T + 1
N_LOADS_A, N_LOADS_B = 5, 9
OWN = (slice(0, XD), slice(XD, 2 * XD))
OTHER = OWN[::-1]
TOKENS = (slice(0, S), slice(M, KEYS))
MEMORIES = (slice(S, KEYS), slice(0, M))
MEM, Q, K, V = range(4)
A_PJ, V_PJ, G_PJ = 7, 10, 2
A_Q, A_K = 3, 6
V_MEM = 6


def decoder_layer(nc, x, ctx, wq, bq, wk, bk, wv, bv, wo, bo, rel, ln_g, ln_b, xwq, xwkv, xwm, xwo, xbo,
                  wg, we, be, out):
    with ExitStack() as stack:
        def sb(name, shape, dt=F32):
            return stack.enter_context(nc.sbuf_tensor(name, shape, dt))

        def sem(name):
            return stack.enter_context(nc.semaphore(name))

        ident = sb("ident", [P, P])
        ones_row = sb("ones_row", [1, P])
        ones_bf = sb("ones_bf", [P, P], BF16)
        before = sb("before", [P, P], BF16)
        head_mask = sb("head_mask", [P, H])
        quad_mask = sb("quad_mask", [P, 4])
        power = sb("power", [P, TT])
        rank = sb("rank", [P, NE])
        wqkv = sb("wqkv", [P, 3, E])
        wo_sb = sb("wo_sb", [P, E])
        bcols = sb("bcols", [P, 5])
        rows = sb("rows", [1, 3, E])
        rel_sb = sb("rel_sb", [P, REL // P, HD])
        rel_ext = sb("rel_ext", [HD, TW + QI])
        toep = sb("toep", [P, TW])
        xwo_sb = sb("xwo_sb", [P, NP, E])
        ctx_sb = sb("ctx_sb", [NB * M, E])
        ctxT = sb("ctxT", [P, NB * M])
        wg_sb = sb("wg_sb", [P, NE])
        we_sb = sb("we_sb", [P, NE, E])
        weT = sb("weT", [P, NE, E])
        be_sb = sb("be_sb", [NE, E])
        x_sb = [sb(f"x_sb{b}", [P, T, E]) for b in range(NB)]
        xT = sb("xT", [P, S])
        qT = [sb(f"qT{b}", [P, S]) for b in range(NB)]
        kT = [sb(f"kT{b}", [P, S]) for b in range(NB)]
        v_sb = [sb(f"v_sb{b}", [P, T, E]) for b in range(NB)]
        q_rep = sb("q_rep", [NB * QI * HD, H, S])
        q_heads = [sb(f"q_heads{k}", [P, GI, H]) for k in range(2)]
        q_pos = [sb(f"q_pos{k}", [P, GI, H]) for k in range(2)]
        prob_a = [sb(f"prob_a{k}", [P, GT, S]) for k in range(2)]
        stat_a = sb("stat_a", [P, 3, 2, GT])
        probT_a = sb("probT_a", [P, T, GT * P])
        o_masked = sb("o_masked", [P, GI, 4])
        outT_a = [sb(f"outT_a{b}", [P, S]) for b in range(NB)]
        z = sb("z", [P, TT, E])
        stats = sb("stats", [P, TT, 6])
        moments = sb("moments", [P, TT, 2])
        var_eps = sb("var_eps", [P, TT])
        rstd = sb("rstd", [P, TT])
        x1 = [sb(f"x1_{b}", [P, T, E]) for b in range(NB)]
        x1n = sb("x1n", [P, T, E])
        x2 = sb("x2", [P, TT, E])
        w_pair = [sb(f"w_pair{k}", [P, 4, P]) for k in range(2)]
        xnT = [sb(f"xnT{b}", [P, S]) for b in range(NB)]
        q_high = [sb(f"q_high{k}", [P, 2, S], F32R) for k in range(2)]
        q_low = [sb(f"q_low{k}", [P, 2, S], F32R) for k in range(2)]
        k_split = [sb(f"k_split{k}", [P, 2, KEYS], F32R) for k in range(2)]
        q_raw, k_raw = sb("q_raw", [P, S]), sb("k_raw", [P, S])
        v_pair = [sb(f"v_pair{k}", [P, T, P]) for k in range(2)]
        vm_pair = [sb(f"vm_pair{k}", [2 * M, P]) for k in range(2)]
        prob_b = [sb(f"prob_b{i}", [P, 2, KEYS]) for i in range(2)]
        stat_b = sb("stat_b", [P, 3, 2])
        probT_b = [sb(f"probT_b{h}", [P, T, P]) for h in range(2)]
        probTm = sb("probTm", [2 * M, P])
        outT_b = sb("outT_b", [P, NP, S])
        x2T = sb("x2T", [P, TT * P])
        lg = sb("lg", [P, TT, NE])
        ex = sb("ex", [P, TT, NE])
        cand = sb("cand", [P, TT, NE])
        chosen = sb("chosen", [P, TT, NE])
        chosen_bf = sb("chosen_bf", [P, TT, NE], BF16)
        coef = sb("coef", [P, TT, NE])
        tok = sb("tok", [P, 5, TT])
        coefT = sb("coefT", [NE, TT * P])
        parts = [probT_a[:, k, :].rearrange("p (e n) -> p e n", n=E) for k in range(3)]
        y_out = sb("y_out", [P, TT, E])

        q_scratch = nc.dram_tensor("q_scratch", (NB, P, S), F32, kind="Internal").ap()

        bank = stack.enter_context(nc.psum_tensor("bank", [P, 8, 512], F32))

        ld_x, ld_q, ld_rel, ld_a, ld_b = [sem("ld_x0"), sem("ld_x1")], sem("ld_q"), sem("ld_rel"), sem("ld_a"), sem("ld_b")
        ld_pair = [sem("ld_pair0"), sem("ld_pair1")]
        sc_w, sc_r = sem("scratch_written"), sem("q_rep_loaded")
        g_const, v_set, pe_set, a_set = sem("g_const"), sem("v_set"), sem("pe_set"), sem("a_set")
        ld_toep = sem("toeplitz_loaded")
        pe_prep, v_prep, a_prep = sem("pe_prep"), sem("v_prep"), sem("a_prep")
        g_build = sem("g_build")
        pe_sa, v_maxa, a_expa, v_rca, v_na = sem("pe_scores_a"), sem("v_max_a"), sem("a_exp_a"), sem("v_recip_a"), sem("v_norm_a")
        pe_tra, v_eva, a_eva, pe_pva, v_oa = sem("pe_transposed_a"), sem("v_evac_a"), sem("a_evac_a"), sem("pe_pv_a"), sem("v_out_a")
        pe_wo, v_za, v_zb, v_ln, g_pow = sem("pe_wo"), sem("v_resid_a"), sem("v_resid_b"), sem("v_ln"), sem("g_pow")
        pe_xn, a_xn = sem("pe_xn"), sem("a_xn")
        pe_pj, a_pj, v_pj, g_pj = sem("pe_proj"), sem("a_proj"), sem("v_proj"), sem("g_proj")
        pe_sb, v_maxb, a_expb, v_rcb, v_nb, g_nb = sem("pe_scores_b"), sem("v_max_b"), sem("a_exp_b"), sem("v_recip_b"), sem("v_norm_b"), sem("g_norm_b")
        pe_trb, v_evb, v_evm, a_evb, pe_pvb, a_ob = sem("pe_transposed_b"), sem("v_evac_b"), sem("v_evac_mem"), sem("a_evac_b"), sem("pe_pv_b"), sem("a_out_b")
        pe_wob = sem("pe_wo_b")
        pe_m, v_m, a_m = sem("pe_moe"), sem("v_moe"), sem("a_moe")
        pe_y, v_gate, v_acc, v_fin, v_lnf = sem("pe_expert"), sem("v_gate"), sem("v_acc"), sem("v_finish"), sem("v_stats_final")
        v_lnm, a_part, g_sum = sem("v_ln_final"), sem("a_part"), sem("g_sum")
        g_powf, st_out = sem("g_pow_final"), sem("stored")

        x_rows = x.rearrange("b (t p) e -> b p t e", p=P)
        out_rows = out.rearrange("b (t p) e -> p (b t) e", p=P)

        passed = {name: sem(f"passed_{name}") for name in ("pool", "pe", "dve")}

        def stand_alone(eng, name):
            eng.sem_inc(passed[name])

        block = stack.enter_context(nc.Block())

        @block.sync
        def _(sp):
            sp.dma_start(x_sb[0][:], x_rows[0]).then_inc(ld_x[0], 16)
            sp.dma_start(wqkv[:, 0, :], wq).then_inc(ld_q, 16)
            sp.dma_start(bcols[:, 0:1], bq.rearrange("(p a) -> p a", a=1)).then_inc(ld_q, 16)
            sp.dma_start(wqkv[:, 1, :], wk).then_inc(ld_a, 16)
            sp.dma_start(wqkv[:, 2, :], wv).then_inc(ld_a, 16)
            sp.dma_start(bcols[:, 1:2], bk.rearrange("(p a) -> p a", a=1)).then_inc(ld_a, 16)
            sp.dma_start(rows[:, 0, :], bv.rearrange("(a n) -> a n", a=1)).then_inc(ld_a, 16)
            sp.dma_start(rows[:, 1, :], bo.rearrange("(a n) -> a n", a=1)).then_inc(ld_a, 16)
            for b in range(NB):
                sp.wait_ge(a_prep, b + 1)
                sp.dma_start(q_scratch[b], qT[b][:]).then_inc(sc_w, 16)
                sp.wait_ge(sc_w, 16 * (b + 1))
                for i in range(b * QI, (b + 1) * QI):
                    sp.dma_start(q_rep[HD * i:HD * (i + 1), :, :],
                                 q_scratch[b].rearrange("(h d) i -> d h i", d=HD)).then_inc(sc_r, 16)
                if b == 0:
                    sp.dma_start(x_sb[1][:], x_rows[1]).then_inc(ld_x[1], 16)
                    sp.dma_start(wo_sb[:], wo).then_inc(ld_b, 16)
                    sp.dma_start(xwo_sb[:], xwo.rearrange("(c p) n -> p c n", p=P)).then_inc(ld_b, 16)
                    sp.dma_start(rows[:, 2, :], xbo.rearrange("(a n) -> a n", a=1)).then_inc(ld_b, 16)
                    sp.dma_start(bcols[:, 2:3], ln_g.rearrange("(p a) -> p a", a=1)).then_inc(ld_b, 16)
                    sp.dma_start(bcols[:, 3:4], ln_b.rearrange("(p a) -> p a", a=1)).then_inc(ld_b, 16)
                    sp.dma_start(ctx_sb[:], ctx.rearrange("b m e -> (b m) e")).then_inc(ld_b, 16)
                    sp.dma_start(wg_sb[:], wg).then_inc(ld_b, 16)
                    sp.dma_start(we_sb[:], we.rearrange("e f h -> f e h")).then_inc(ld_b, 16)
                    sp.dma_start(be_sb[:], be).then_inc(ld_b, 16)

            def load_pair(p, k):
                for j, src in enumerate((xwq[:, bass.ds(p * P, P)], xwkv[:, bass.ds(p * P, P)],
                                         xwkv[:, bass.ds(p * P + NP * P, P)], xwm[:, bass.ds(p * P, P)])):
                    sp.dma_start(w_pair[k][:, j, :], src).then_inc(ld_pair[k], 16)

            load_pair(0, 0)
            load_pair(1, 1)
            for b in range(NB):
                with sp.Fori(1 - b, NP // 2) as r:
                    for k in range(2):
                        sp.wait_ge(pe_pj, r * 8 + (b * 4 * NP + 4 * (k - 1)))
                        load_pair(r * 2 + k, k)
            for n in range(NB):
                sp.wait_ge(v_lnm, LN_MORE * (n + 1))
                sp.dma_start(out_rows[:, T * n:T * (n + 1), :], y_out[:, T * n:T * (n + 1), :]).then_inc(st_out, 16)
            sp.wait_ge(st_out, 16 * NB)

        @block.gpsimd
        def _(pool):
            def masked(out, base, mult, pattern, op, fill, n):
                pool.wait_ge(g_const, n)
                pool.affine_select(out=out, in_=out, compare_op=op, fill=fill, base=base, pattern=pattern,
                                   channel_multiplier=mult).then_inc(g_const, 1)

            pool.memset(ident[:], 0.0).then_inc(g_const, 1)
            masked(ident[:], 0, 1, [[-1, P]], ALU.not_equal, 1.0, 1)
            pool.memset(head_mask[:], 1.0).then_inc(g_const, 1)
            masked(head_mask[:], 0, 1, [[-HD, H]], ALU.is_ge, 0.0, 3)
            masked(head_mask[:], HD - 1, -1, [[HD, H]], ALU.is_ge, 0.0, 4)
            pool.memset(toep[:], 0.0).then_inc(g_const, 1)
            masked(toep[:], WIN - QI * HD, 1, [[-1, TW]], ALU.is_ge, NEG, 6)
            for k in range(2):
                pool.memset(q_pos[k][:], 0.0).then_inc(g_const, 1)
            pool.memset(ones_row[:], 1.0).then_inc(g_const, 1)
            for k in range(2):
                masked(q_pos[k][:].rearrange("p (t i) h -> p t i h", i=QI), -QI * HD, 1,
                       [[0, GT], [-1, QI], [0, H]], ALU.not_equal, 1.0, 9)
            pool.memset(power[:], -0.5).then_inc(g_const, 1)
            pool.memset(ones_bf[:], 1.0).then_inc(g_const, 1)
            pool.memset(before[:], 1.0).then_inc(g_const, 1)
            masked(before[:], -1, -1, [[1, P]], ALU.is_ge, 0.0, 15)
            pool.iota(rank[:], [[-1, NE]], base=NE, channel_multiplier=0, allow_small_or_imprecise_dtypes=True).then_inc(g_const, 1)

            def build(gg):
                k, b, g = gg % 2, gg // G, gg % G
                if g == 0:
                    pool.wait_ge(a_prep, b + 1)
                if gg >= 2:
                    pool.wait_ge(pe_sa, GT * (gg - 1))
                cols = qT[b][:, GI * g:GI * (g + 1)].unsqueeze(2).broadcast_to([P, GI, H])
                pool.tensor_tensor(q_heads[k][:], cols, head_mask[:].unsqueeze(1).broadcast_to([P, GI, H]),
                                   ALU.mult).then_inc(g_build, 1)
                if g == 0:
                    pool.wait_ge(sc_r, 16 * QI * (b + 1))
                if b > 0:
                    pool.wait_ge(g_build, 2 * gg + 1)
                n = QI * HD
                part = slice(n * b, n * (b + 1))
                rep = q_rep[part, :, GI * g:GI * (g + 1)].rearrange("p h (t i) -> p t i h", i=QI)
                pick = head_mask[part, QI * b:QI * (b + 1)].unsqueeze(1).unsqueeze(3).broadcast_to([n, GT, QI, H])
                pool.tensor_tensor(q_pos[k][0:n].rearrange("p (t i) h -> p t i h", i=QI), rep, pick,
                                   ALU.mult).then_inc(g_build, 1)
                if b > 0:
                    pool.wait_ge(g_build, 2 * gg + 2)

            def rsqrt(n):
                pool.wait_ge(v_ln, LN * n + LN_BEGIN)
                pool.tensor_tensor(rstd[:, 0:T], var_eps[:, 0:T], power[:, 0:T], ALU.pow).then_inc(g_pow, 1)
                pool.wait_ge(g_pow, n + 1)

            def normalise(u, i):
                pool.wait_ge(v_rcb, u * 2 + 1)
                stand_alone(pool, "pool")
                row = prob_b[i][:, 0, :]
                pool.tensor_scalar(row, row, stat_b[:, 2, 0:1], 1.0, ALU.mult,
                                   ALU.mult).then_inc(g_nb, 1)

            for gg in range(NB * G):
                if gg == LN_0 + 3:
                    rsqrt(0)
                if gg == LN_1 + 3:
                    rsqrt(1)
                build(gg)
            def split_q(pg, k):
                pool.wait_ge(a_pj, pg * A_PJ + A_Q)
                for h in range(2):
                    if h == 1:
                        pool.wait_ge(g_pj, pg * G_PJ + 1)
                    stand_alone(pool, "pool")
                    pool.tensor_tensor(q_low[k][OWN[h], h, :], q_raw[OWN[h], :], q_high[k][OWN[h], h, :].bitcast(F32),
                                       ALU.subtract).then_inc(g_pj, 1)
                pool.wait_ge(g_pj, pg * G_PJ + 2)

            def unit(pg, k, it, slot=None):
                u = pg * 4 + it
                if slot != NB * NU - 1:
                    normalise(u + 1, 1 - it % 2)
                if it == 1 and (slot is None or slot < NB * NU - T):
                    pool.wait_ge(g_nb, u + 2)
                    split_q(pg + 1, 1 - k)
                if slot in (0, 1):
                    rsqrt(2 + slot)
                if slot == NU:
                    rsqrt(4)

            split_q(0, 0)
            normalise(0, 0)
            for b in range(NB):
                for it in range(T):
                    unit(b * NP, 0, it, b * NU + it)
                with pool.Fori(0, NP // 2 - 1) as r:
                    for k in (1, 0):
                        for it in range(T):
                            unit(r * 2 + (b * NP + 2 - k), k, it)
                for it in range(T):
                    unit(b * NP + NP - 1, 1, it, b * NU + NU - T + it)
            rsqrt(5)
            for t in range(TT):
                part = parts[t % 3]
                pool.wait_ge(a_part, 4 * (t + 1))
                pool.tensor_tensor(part[:, 0:2, :], part[:, 0:2, :], part[:, 2:4, :], ALU.add).then_inc(g_sum, 1)
                pool.wait_ge(g_sum, 2 * t + 1)
                pool.tensor_tensor(part[:, 0, :], part[:, 0, :], part[:, 1, :], ALU.add).then_inc(g_sum, 1)
                if t == 5 or t == TT - 1:
                    b = int(t == TT - 1)
                    pool.wait_ge(v_lnm, LN_MORE * b + T + 1)
                    pool.tensor_tensor(rstd[:, T * b:T * (b + 1)], var_eps[:, T * b:T * (b + 1)],
                                       power[:, 0:T], ALU.pow).then_inc(g_powf, 1)

        @block.scalar
        def _(act):
            def copy(out, in_, done):
                act.activation(out, in_, ACT.Copy).then_inc(done, 1)

            act.dma_start(rel_sb[:], rel.rearrange("(c p) d -> p c d", p=P)).then_inc(ld_rel, 16)

            act.wait_ge(pe_set, 1)
            r_cols = bank[0:HD, 0, 0:REL]
            copy(rel_ext[:, REL:2 * REL], r_cols, a_set)
            act.activation(rel_ext[:, 0:REL], r_cols[:, 0:1].broadcast_to([HD, REL]), ACT.Copy).then_inc(a_set, 1)
            rest = TW + QI - 2 * REL
            act.activation(rel_ext[:, 2 * REL:], r_cols[:, REL - 1:REL].broadcast_to([HD, rest]), ACT.Copy).then_inc(a_set, 1)
            def prep_q(b, n):
                act.wait_ge(pe_prep, 4 * b + 2)
                act.activation(qT[b][:], bank[:, n, :], ACT.Identity, bias=bcols[:, 4:5],
                               scale=SCALE_A).then_inc(a_prep, 1)

            def xn_evac(b):
                act.wait_ge(pe_xn, b + 1)
                act.activation(xnT[b][:], bank[:, 7, :], ACT.Identity, bias=bcols[:, 3:4],
                               scale=bcols[:, 2:3]).then_inc(a_xn, 1)

            def exp_a(gg, t):
                act.wait_ge(v_maxa, GT * gg + t + 1)
                n = GI * (gg % G + 1)
                act.activation(prob_a[gg % 2][:, t, 0:n], bank[:, t, 0:n], ACT.Exp,
                               bias=stat_a[:, 0, gg % 2, t:t + 1], scale=1.0,
                               accum_out=stat_a[:, 1, gg % 2, t:t + 1]).then_inc(a_expa, 1)

            def piece(pg, k, j):
                act.wait_ge(pe_pj, pg * 4 + (j + 1))
                if j == Q:
                    act.activation(q_raw[:], bank[:, 7, :], ACT.Copy, scale=SCALE_B).then_inc(a_pj, 1)
                    for h in range(2):
                        act.activation(q_high[k][OWN[h], h, :], bank[OWN[h], 7, :], ACT.Copy,
                                       scale=SCALE_B).then_inc(a_pj, 1)
                if j == K:
                    copy(k_raw[:], bank[:, 7, :], a_pj)
                    for h in range(2):
                        copy(k_split[k][OWN[h], h, TOKENS[h]], bank[OWN[h], 7, :], a_pj)
                if j == V:
                    copy(v_pair[k][:], bank[:, 7, :].rearrange("p (t n) -> p t n", n=P), a_pj)

            def exp_b(u, h, i):
                act.wait_ge(v_maxb, u * 2 + (h + 1))
                act.activation(prob_b[i][:, h, :].rearrange("p (c n) -> p c n", c=2), bank[:, 2 * h:2 * h + 2, 0:KH],
                               ACT.Exp, bias=stat_b[:, 0, h:h + 1], scale=1.0,
                               accum_out=stat_b[:, 1, h:h + 1]).then_inc(a_expb, 1)

            act.wait_ge(v_set, 1)
            prep_q(0, 4)
            act.wait_ge(a_set, 3)
            act.wait_ge(g_const, 7)
            for i in range(QI):
                act.dma_start(toep[HD * i:HD * (i + 1), :],
                             rel_ext[:, QI - 1 - i:QI - 1 - i + TW]).then_inc(ld_toep, 16)
            for t in range(GT):
                exp_a(0, t)
            for gg in range(NB * G):
                if gg == PREP_1[1]:
                    prep_q(1, 7)
                if gg in SETUP:
                    n = SETUP.index(gg)
                    act.wait_ge(pe_set, n + 2)
                    if n < 2:
                        copy(weT[:, 4 * n:4 * n + 4, :], bank[:, 7, :].rearrange("p (e f) -> p e f", f=E), a_set)
                    else:
                        copy(ctxT[:], bank[:, 7, 0:NB * M], a_set)
                if gg == XN_0:
                    act.wait_ge(ld_b, 16 * N_LOADS_B)
                    xn_evac(0)
                if gg in PIECES_0[Q:]:
                    piece(0, 0, PIECES_0.index(gg))
                if gg + 1 < NB * G:
                    exp_a(gg + 1, 0)
                for t in range(GT):
                    if gg + 1 < NB * G and t < GT - 1:
                        exp_a(gg + 1, t + 1)
                    if gg == NB * G - 1 and t < 2:
                        exp_b(0, t, 0)
                    n = gg // G * NTR + TR0[gg % G] + t
                    if t < chunks(gg % G) and n % 2 == 1:
                        rows_n = min(P, GI * (gg % G + 1) - P * t)
                        act.wait_ge(pe_tra, n + 1)
                        copy(probT_a[0:rows_n, t, :], bank[0:rows_n, 5, :], a_eva)

            def unit(pg, k, it, slot=None):
                u = pg * 4 + it
                last = slot == NB * NU - 1
                act.wait_ge(pe_trb, u * 2 + 2)
                copy(probT_b[1][:], bank[:, 5, :].rearrange("p (c n) -> p c n", n=P), a_evb)
                if not last:
                    exp_b(u + 1, 0, 1 - it % 2)
                    exp_b(u + 1, 1, 1 - it % 2)
                act.wait_ge(pe_pvb, u + 1)
                p = slot // T % NP if slot is not None else pg - pg_row[0]
                copy(outT_b[:, bass.ds(p, 1), it * P:(it + 1) * P], bank[:, 6, 0:P].unsqueeze(1), a_ob)
                if it != 2 and (slot is None or slot < NB * NU - T):
                    piece(pg + 1, 1 - k, (Q, K, None, V)[it])
                if slot == 3:
                    xn_evac(1)

            pg_row = [0]
            for b in range(NB):
                pg_row[0] = b * NP
                for it in range(T):
                    unit(b * NP, 0, it, b * NU + it)
                with act.Fori(0, NP // 2 - 1) as r:
                    for k in (1, 0):
                        for it in range(T):
                            unit(r * 2 + (b * NP + 2 - k), k, it)
                for it in range(T):
                    unit(b * NP + NP - 1, 1, it, b * NU + NU - T + it)

            for b in range(NB):
                act.wait_ge(pe_m, 2 * b + 1)
                copy(x2T[:, b * S:(b + 1) * S], bank[:, b, :], a_m)
            act.wait_ge(v_m, 2)
            act.activation(ex[:], lg[:], ACT.Exp).then_inc(a_m, 1)
            act.wait_ge(v_m, 10)

            def scaled_parts(t):
                act.wait_ge(pe_y, t + 1)
                if t >= 3:
                    act.wait_ge(v_fin, 2 * (t - 3) + 1)
                for e in range(4):
                    act.activation(parts[t % 3][:, e, :], bank[:, EXPERT_BANKS[t % 3] + 1, e * E:(e + 1) * E], ACT.Copy,
                                   scale=coef[:, t, 4 + e:5 + e]).then_inc(a_part, 1)

            scaled_parts(0)
            act.wait_ge(pe_m, 6)
            for b in range(NB):
                copy(coefT[:, b * S:(b + 1) * S], bank[0:NE, 4 + b, :], a_m)
            for t in range(1, TT):
                scaled_parts(t)

        @block.tensor
        def _(pe):
            def transpose_to(out, in_, k=P):
                return pe.transpose(out, in_, ident[0:k, 0:k])

            def add_bias(n, row):
                return pe.matmul(bank[:, n, :], ones_row[:], rows[:, row, :].unsqueeze(1).broadcast_to([1, T, E]),
                                 start=False, stop=True, skip_group_check=True)

            pe.wait_ge(ld_rel, 16)
            pe.wait_ge(g_const, 2)
            for c in range(REL // P):
                last = transpose_to(bank[0:HD, 0, c * P:(c + 1) * P], rel_sb[:, c, :])
            last.then_inc(pe_set, 1)

            def setup(n):
                if n == 0:
                    pe.wait_ge(ld_b, 16 * N_LOADS_B)
                    pe.wait_ge(v_prep, 6)
                else:
                    pe.wait_ge(a_set, n + 3)
                if n < 2:
                    for e in range(4):
                        last = transpose_to(bank[:, 7, e * E:(e + 1) * E], we_sb[:, 4 * n + e, :])
                else:
                    last = transpose_to(bank[:, 7, 0:NB * M], ctx_sb[:], NB * M)
                last.then_inc(pe_set, 1)

            def prep_x(b):
                pe.wait_ge(ld_x[b], 16)
                for t in range(T):
                    last = transpose_to(bank[:, 7, t * P:(t + 1) * P], x_sb[b][:, t, :])
                last.then_inc(pe_prep, 1)

            def prep(b, j, n):
                if j < 2:
                    pe.matmul(bank[:, n, :], wqkv[:, j, :], xT[:], start=True, stop=True).then_inc(pe_prep, 1)
                else:
                    for t in range(T):
                        pe.matmul(bank[:, n, t * E:(t + 1) * E], xT[:, t * P:(t + 1) * P], wqkv[:, 2, :],
                                  start=(t == 0), stop=False, skip_group_check=True)
                    add_bias(n, 0).then_inc(pe_prep, 1)

            def scores_a(gg, t):
                b, g = gg // G, gg % G
                if t == 0:
                    pe.wait_ge(g_build, 2 * (gg + 1))
                if g == 0 and t == 0:
                    pe.wait_ge(v_prep, b * 3 + 2)
                if gg == 0 and t == 0:
                    pe.wait_ge(ld_toep, 16 * QI)
                if gg > 0:
                    pe.wait_ge(a_expa, GT * (gg - 1) + t + 1)
                n = GI * (g + 1)
                first = WIN - (GI * g + QI * t)
                tile = slice(QI * t, QI * (t + 1))
                pe.matmul(bank[:, t, 0:n], q_heads[gg % 2][:, tile, :], kT[b][:, 0:n], start=True, stop=False)
                pe.matmul(bank[:, t, 0:n], q_pos[gg % 2][:, tile, :], toep[:, first:first + n],
                          start=False, stop=True).then_inc(pe_sa, 1)

            def evacuated(n):
                pe.wait_ge((v_eva, a_eva)[n % 2], n // 2 + 1)

            def transposes_a(gg, c):
                g = gg % G
                n = gg // G * NTR + TR0[g] + c
                if c == 0:
                    pe.wait_ge(v_na, GT * (gg + 1))
                if gg == 0 and c == 0:
                    pe.wait_ge(a_prep, 1)
                    pe.wait_ge(v_prep, 3)
                if n >= 2:
                    evacuated(n - 2)
                rows_n = min(P, GI * (g + 1) - P * c)
                for t in range(GT):
                    last = transpose_to(bank[0:rows_n, 4 + n % 2, t * P:(t + 1) * P],
                                        prob_a[gg % 2][:, t, c * P:c * P + rows_n])
                last.then_inc(pe_tra, 1)

            def pv_a(gg, c):
                b, g = gg // G, gg % G
                evacuated(b * NTR + TR0[g] + c)
                if c == 0 and gg > 0:
                    pe.wait_ge(v_oa, 2 * (gg - 1) + 1)
                if gg == G and c == 0:
                    pe.wait_ge(v_prep, 6)
                rows_n = min(P, GI * (g + 1) - P * c)
                for q in range(4):
                    moving = probT_a[0:rows_n, c, :].rearrange("p (i h) -> p i h", h=H)[:, :, 4 * q:4 * q + 4]
                    last = pe.matmul(bank[32 * q:32 * q + 32, 6, 0:P], v_sb[b][0:rows_n, c, 32 * q:32 * q + 32],
                                     moving, start=(c == 0), stop=(c == chunks(g) - 1),
                                     tile_position=(0, 32 * q))
                if c == chunks(g) - 1:
                    last.then_inc(pe_pva, 1)

            def wo_a(b):
                pe.wait_ge(v_oa, 2 * G * (b + 1))
                for t in range(T):
                    pe.matmul(bank[:, 7, t * E:(t + 1) * E], outT_a[b][:, t * P:(t + 1) * P], wo_sb[:],
                              start=(t == 0), stop=False, skip_group_check=True)
                add_bias(7, 1).then_inc(pe_wo, 1)

            def xn_transposes(b):
                pe.wait_ge(v_ln, LN * (2 * b + 2))
                for t in range(T):
                    last = transpose_to(bank[:, 7, t * P:(t + 1) * P], x1n[:, t, :])
                last.then_inc(pe_xn, 1)

            def piece(pg, k, row, j, n=7, tiles=range(T)):
                first = isinstance(pg, int) and pg == 0
                if j == MEM:
                    memories = ctxT[:, row * M:(row + 1) * M]
                    pe.wait_ge(ld_pair[k], pg * 32 + (2 - k) * 32)
                    pe.matmul(bank[:, n, 2 * P:2 * P + M], w_pair[k][:, 3, :], memories, start=True, stop=True)
                    pe.matmul(bank[0:M, n, 3 * P:4 * P], memories, w_pair[k][:, 3, :], start=True,
                              stop=True).then_inc(pe_pj, 1)
                if j == Q:
                    if not first:
                        pe.wait_ge(a_pj, pg * A_PJ)
                    pe.matmul(bank[:, n, :], w_pair[k][:, 0, :], xnT[row][:], start=True, stop=True).then_inc(pe_pj, 1)
                if j == K:
                    pe.wait_ge(a_pj, pg * A_PJ + A_Q)
                    pe.matmul(bank[:, n, :], w_pair[k][:, 1, :], xnT[row][:], start=True, stop=True).then_inc(pe_pj, 1)
                if j == V:
                    if tiles[0] == 0:
                        pe.wait_ge(a_pj, pg * A_PJ + A_K)
                    for t in tiles:
                        last = pe.matmul(bank[:, n, t * P:(t + 1) * P], xnT[row][:, t * P:(t + 1) * P],
                                         w_pair[k][:, 2, :], start=True, stop=True)
                    if tiles[-1] == T - 1:
                        last.then_inc(pe_pj, 1)

            def scores_b(pg, k, it, h, u=None):
                if h == 0 and u is not None:
                    pe.wait_ge(a_expb, u * 2 + 1)
                if it == 0 and h == 0:
                    pe.wait_ge(v_pj, pg * V_PJ + V_PJ)
                    pe.wait_ge(g_pj, pg * G_PJ + G_PJ)
                for c in range(2):
                    for q in (q_high, q_low):
                        last = pe.matmul(bank[:, 2 * h + c, 0:KH], q[k][:, h, it * P:(it + 1) * P],
                                         k_split[k][:, h, c * KH:(c + 1) * KH], start=(q is q_high), stop=(q is q_low))
                last.then_inc(pe_sb, 1)

            prep_x(0)
            pe.wait_ge(v_prep, 1)
            pe.wait_ge(ld_q, 2 * 16)
            prep(0, 0, 4)
            pe.wait_ge(ld_a, 16 * N_LOADS_A)
            prep(0, 1, 5)
            pe.wait_ge(g_const, 10)
            prep(0, 2, 6)
            pe.wait_ge(a_set, 3)
            for t in range(GT):
                scores_a(0, t)
            for gg in range(NB * G):
                if gg == PREP_1[0]:
                    prep_x(1)
                if gg == PREP_1[1]:
                    pe.wait_ge(v_prep, 4)
                    prep(1, 0, 7)
                if gg == PREP_1[2]:
                    pe.wait_ge(a_prep, 2)
                    prep(1, 1, 7)
                if gg == PREP_1[3]:
                    pe.wait_ge(v_prep, 5)
                    prep(1, 2, 7)
                if gg in SETUP:
                    setup(SETUP.index(gg))
                if gg == WO_0:
                    pe.wait_ge(a_set, 6)
                    wo_a(0)
                if gg == XN_0:
                    xn_transposes(0)
                if gg in PIECES_0:
                    if gg == PIECES_0[0]:
                        pe.wait_ge(a_xn, 1)
                    if gg == PIECES_0[Q]:
                        pe.wait_ge(v_pj, V_MEM)
                    piece(0, 0, 0, PIECES_0.index(gg))
                if gg + 1 < NB * G:
                    scores_a(gg + 1, 0)
                if gg > 0:
                    pv_a(gg - 1, chunks((gg - 1) % G) - 1)
                if gg == NB * G - 1:
                    pe.wait_ge(v_set, 8)
                    pe.wait_ge(a_expa, NB * G * GT)
                for t in range(GT):
                    if gg + 1 < NB * G and t < GT - 1:
                        scores_a(gg + 1, t + 1)
                    if gg == NB * G - 1 and t < 2:
                        scores_b(0, 0, 0, t)
                    if t < chunks(gg % G):
                        transposes_a(gg, t)
                    if 1 <= t < chunks(gg % G):
                        pv_a(gg, t - 1)
            pv_a(NB * G - 1, chunks(G - 1) - 1)

            def wo_b(pairs, tiles):
                for p in pairs:
                    for t in tiles:
                        pe.matmul(bank[:, 7, t * E:(t + 1) * E], outT_b[:, p, t * P:(t + 1) * P],
                                  xwo_sb[:, p, :], start=(p == 0 and t == 0), stop=False, skip_group_check=True)

            def unit(pg, k, row, it, slot=None):
                u = pg * 4 + it

                def next_scores(h):
                    if it < T - 1:
                        scores_b(pg, k, it + 1, h, u)
                    elif slot != NB * NU - 1:
                        scores_b(pg + 1, 1 - k, 0, h, u)

                next_scores(0)
                for h in range(2):
                    if slot == 0 and h == 0:
                        evacuated(NB * NTR - 2)
                        evacuated(NB * NTR - 1)
                        pe.wait_ge(v_oa, 2 * NB * G)
                    pe.wait_ge((g_nb, v_nb)[h], u + 1)
                    if h == 1 and slot != 0:
                        pe.wait_ge(a_ob, u)
                    stand_alone(pe, "pe")
                    for c in range(T):
                        last = transpose_to(bank[:, 4 + h, c * P:(c + 1) * P], prob_b[it % 2][:, h, TOKENS[h].start + c * P:TOKENS[h].start + (c + 1) * P])
                    if h == 1 and it == 0 and (slot is None or slot < NB * NU - T):
                        piece(pg + 1, 1 - k, (slot + T) // NU if slot is not None else row, MEM, 6)
                    if h == 1:
                        last = transpose_to(bank[0:2 * M, 6, P:2 * P], prob_b[it % 2][:].rearrange("p h n -> p (h n)")[:, S:S + 2 * M])
                    last.then_inc(pe_trb, 1)
                    if slot == 0 and h == 0:
                        pe.wait_ge(a_pj, A_PJ)
                        wo_a(1)
                    if slot == NU and h == 0:
                        pe.wait_ge(a_pj, (NP + 1) * A_PJ)
                        pe.wait_ge(a_ob, NU)
                        wo_b(range(NP), range(T))
                        add_bias(7, 2).then_inc(pe_wob, 1)
                next_scores(1)
                if slot == 0:
                    pe.wait_ge(v_za, 2)
                if slot == NU:
                    pe.wait_ge(v_zb, 1)
                if slot is None or slot < NB * NU - T:
                    piece(pg + 1, 1 - k, (slot + T) // NU if slot is not None else row, (Q, K, V, V)[it],
                          tiles=range(2 * it - 4, 2 * it - 2) if it > 1 else ())
                else:
                    if it == 0:
                        pe.wait_ge(a_pj, NB * NP * A_PJ)
                        pe.wait_ge(a_ob, u)
                    wo_b(range(NP - 1), (it, ))
                pe.wait_ge(v_evb, u + 1)
                pe.wait_ge(v_evm, u + 1)
                pe.wait_ge(a_evb, u + 1)
                if it == 0:
                    pe.wait_ge(a_pj, pg * A_PJ + A_PJ)
                    if slot is None or slot < NB * NU - T:
                        pe.wait_ge(v_pj, (pg + 1) * V_PJ + V_MEM)
                pe.matmul(bank[:, 6, 0:P], vm_pair[k][:], probTm[:], start=True, stop=False, skip_group_check=True)
                for c in range(T):
                    for h in range(2):
                        last = pe.matmul(bank[OWN[h], 6, 0:P], v_pair[k][:, c, OWN[h]], probT_b[h][:, c, :],
                                         start=False, stop=(c == T - 1), tile_position=(0, XD * h), skip_group_check=True)
                last.then_inc(pe_pvb, 1)
                if slot == 3:
                    pe.wait_ge(a_pj, 2 * A_PJ)
                    xn_transposes(1)
                    pe.wait_ge(a_xn, 2)

            for b in range(NB):
                for it in range(T):
                    unit(b * NP, 0, b, it, b * NU + it)
                with pe.Fori(0, NP // 2 - 1) as r:
                    for k in (1, 0):
                        for it in range(T):
                            unit(r * 2 + (b * NP + 2 - k), k, b, it)
                for it in range(T):
                    unit(b * NP + NP - 1, 1, b, it, b * NU + NU - T + it)

            pe.wait_ge(a_ob, NB * NU)
            wo_b((NP - 1, ), range(T))
            add_bias(7, 2).then_inc(pe_wob, 1)

            for b in range(NB):
                pe.wait_ge(v_ln, (len(LNS) - 1 + b) * LN)
                for t in range(T):
                    last = transpose_to(bank[:, b, t * P:(t + 1) * P], x2[:, b * T + t, :])
                last.then_inc(pe_m, 1)
                pe.wait_ge(a_m, b + 1)
                for t in range(b * T, (b + 1) * T):
                    last = pe.matmul(bank[:, 4, t * NE:(t + 1) * NE], x2T[:, t * P:(t + 1) * P], wg_sb[:],
                                     start=True, stop=True)
                last.then_inc(pe_m, 1)

            def experts(t):
                if t >= 3:
                    pe.wait_ge(v_acc, 4 * (t - 2))
                    pe.wait_ge(a_part, 4 * (t - 2))
                for c in range(2):
                    last = pe.matmul(bank[:, EXPERT_BANKS[t % 3] + c, :], x2T[:, t * P:(t + 1) * P],
                                     weT[:, 4 * c:4 * c + 4, :].rearrange("p e f -> p (e f)"), start=True, stop=True)
                last.then_inc(pe_y, 1)

            experts(0)
            pe.wait_ge(v_m, 8)
            pe.wait_ge(g_const, 17)
            for t in range(TT - 1):
                pe.matmul(bank[:, 5, (t + 1) * NE:TT * NE], ones_bf[:],
                          chosen_bf[:, t:t + 1, :].broadcast_to([P, TT - 1 - t, NE]),
                          start=(t == 0), stop=False, skip_group_check=True)
            pe.matmul(bank[:, 5, 0:TT * NE], before[:], chosen_bf[:].rearrange("p t e -> p (t e)"),
                      start=False, stop=True, skip_group_check=True).then_inc(pe_m, 1)
            experts(1)
            pe.wait_ge(v_zb, NB)
            experts(2)
            pe.wait_ge(v_m, 10)
            for t in range(TT):
                last = transpose_to(bank[0:NE, 4 + t // 4, (t % 4) * P:(t % 4 + 1) * P], coef[:, t, :])
            last.then_inc(pe_m, 1)
            pe.wait_ge(a_m, 5)
            for t in range(TT):
                last = pe.matmul(bank[:, 4 + t // 4, (t % 4) * P:(t % 4 + 1) * P], coefT[:, t * P:(t + 1) * P],
                                 be_sb[:], start=True, stop=True)
            last.then_inc(pe_m, 1)
            for t in range(3, TT):
                experts(t)

        @block.vector
        def _(dve):
            dve.wait_ge(ld_q, 2 * 16)
            dve.tensor_scalar(bcols[:, 4:5], bcols[:, 0:1], SCALE_A, None, ALU.mult).then_inc(v_set, 1)
            dve.wait_ge(g_const, 5)
            dve.tensor_reduce(quad_mask[:], head_mask[:].rearrange("p (c q) -> p q c", q=4), AX.X,
                              ALU.add).then_inc(v_set, 1)

            def prep_x(b):
                dve.wait_ge(pe_prep, b * 4 + 1)
                dve.tensor_copy(xT[:], bank[:, 7, :]).then_inc(v_prep, 1)

            def prep_k(b, n):
                dve.wait_ge(pe_prep, b * 4 + 3)
                dve.tensor_scalar(kT[b][:], bank[:, n, :], bcols[:, 1:2], None, ALU.add).then_inc(v_prep, 1)

            def prep_v(b, n):
                dve.wait_ge(pe_prep, b * 4 + 4)
                dve.tensor_copy(v_sb[b][:], bank[:, n, :].rearrange("p (t e) -> p t e", e=E)).then_inc(v_prep, 1)

            def max_a(gg, t):
                dve.wait_ge(pe_sa, GT * gg + t + 1)
                dve.tensor_reduce(stat_a[:, 0, gg % 2, t:t + 1], bank[:, t, 0:GI * (gg % G + 1)], AX.X, ALU.max,
                                  negate=True).then_inc(v_maxa, 1)

            def normalise_a(gg, t):
                dve.wait_ge(a_expa, GT * gg + t + 1)
                dve.reciprocal(stat_a[:, 2, gg % 2, t:t + 1], stat_a[:, 1, gg % 2, t:t + 1]).then_inc(v_rca, 1)
                dve.wait_ge(v_rca, GT * gg + t + 1)
                row = prob_a[gg % 2][:, t, 0:GI * (gg % G + 1)]
                dve.tensor_scalar(row, row, stat_a[:, 2, gg % 2, t:t + 1], None, ALU.mult).then_inc(v_na, 1)

            def ln_begin(i, src):
                v0 = LN * i
                for t in range(T):
                    dve.bn_stats(stats[:, t, :], src[:, t, :]).then_inc(v_ln, 1)
                for t in range(T):
                    dve.wait_ge(v_ln, v0 + t + 1)
                    dve.bn_aggr(moments[:, t, :], stats[:, t, :]).then_inc(v_ln, 1)
                dve.wait_ge(v_ln, v0 + 2 * T)
                dve.tensor_scalar(var_eps[:, 0:T], moments[:, 0:T, 1], EPS, None, ALU.add).then_inc(v_ln, 1)

            def ln_apply(i, src, out):
                dve.wait_ge(g_pow, i + 1)
                for t in range(T):
                    dve.tensor_scalar(out[:, t, :], src[:, t, :], moments[:, t, 0:1], rstd[:, t:t + 1],
                                      ALU.subtract, ALU.mult).then_inc(v_ln, 1)
                dve.wait_ge(v_ln, LN * (i + 1))

            def row_tiles(tile, b):
                return tile[:, b * T:(b + 1) * T, :]

            def residual_a(b):
                dve.wait_ge(pe_wo, b + 1)
                dve.tensor_tensor(row_tiles(z, b), bank[:, 7, :].rearrange("p (t e) -> p t e", e=E), x_sb[b][:],
                                  ALU.add).then_inc(v_za, 1)
                dve.wait_ge(v_za, b + 1)

            def residual_b(b):
                dve.wait_ge(pe_wob, b + 1)
                dve.tensor_tensor(row_tiles(z, b), bank[:, 7, :].rearrange("p (t e) -> p t e", e=E), x1[b][:],
                                  ALU.add).then_inc(v_zb, 1)
                dve.wait_ge(v_zb, b + 1)

            def piece(pg, k, j, n=7):
                if j == MEM:
                    dve.wait_ge(pe_pj, pg * 4 + 1)
                    for h in range(2):
                        dve.tensor_copy(k_split[k][OWN[h], h, MEMORIES[h]], bank[OWN[h], n, 2 * P:2 * P + M]).then_inc(v_pj, 1)
                    for h in range(2):
                        dve.tensor_copy(vm_pair[k][M * h:M * (h + 1), OWN[h]],
                                        bank[0:M, n, 3 * P + XD * h:3 * P + XD * (h + 1)]).then_inc(v_pj, 1)
                    dve.wait_ge(v_pj, pg * V_PJ + 2)
                    stand_alone(dve, "dve")
                    for h in range(2):
                        dve.tensor_tensor(k_split[k][OTHER[h], h, MEMORIES[h]], bank[OWN[h], n, 2 * P:2 * P + M],
                                          k_split[k][OWN[h], h, MEMORIES[h]].bitcast(F32), ALU.subtract).then_inc(v_pj, 1)
                if j == Q:
                    dve.wait_ge(a_pj, pg * A_PJ + 1)
                    for h in range(2):
                        dve.tensor_copy(q_high[k][OTHER[h], h, :], q_raw[OWN[h], :]).then_inc(v_pj, 1)
                if j == K:
                    dve.wait_ge(a_pj, pg * A_PJ + A_K)
                    for h in range(2):
                        dve.tensor_tensor(k_split[k][OTHER[h], h, TOKENS[h]], k_raw[OWN[h], :],
                                          k_split[k][OWN[h], h, TOKENS[h]].bitcast(F32), ALU.subtract).then_inc(v_pj, 1)

            def max_b(u, h):
                dve.wait_ge(pe_sb, u * 2 + (h + 1))
                dve.tensor_reduce(stat_b[:, 0, h:h + 1], bank[:, 2 * h:2 * h + 2, 0:KH], AX.XY, ALU.max,
                                  negate=True).then_inc(v_maxb, 1)

            def recip_b(u, h, i):
                dve.wait_ge(a_expb, u * 2 + (h + 1))
                dve.reciprocal(stat_b[:, 2, h:h + 1], stat_b[:, 1, h:h + 1]).then_inc(v_rcb, 1)
                if h == 1:
                    dve.wait_ge(v_rcb, u * 2 + 2)
                    stand_alone(dve, "dve")
                    dve.tensor_scalar(prob_b[i][:, 1, :], prob_b[i][:, 1, :], stat_b[:, 2, 1:2], None, ALU.mult).then_inc(v_nb, 1)

            def take_out(gg):
                b, g = gg // G, gg % G
                dve.wait_ge(pe_pva, gg + 1)
                dve.tensor_tensor(o_masked[:], bank[:, 6, 0:P].rearrange("p (i q) -> p i q", q=4),
                                  quad_mask[:].unsqueeze(1).broadcast_to([P, GI, 4]), ALU.mult).then_inc(v_oa, 1)
                dve.wait_ge(v_oa, 2 * gg + 1)
                dve.tensor_reduce(outT_a[b][:, GI * g:GI * (g + 1)], o_masked[:], AX.X, ALU.add).then_inc(v_oa, 1)

            prep_x(0)
            prep_k(0, 5)
            prep_v(0, 6)
            for k in range(2):
                for h in range(2):
                    dve.memset(q_low[k][OTHER[h], h, :].bitcast(F32), 0.0).then_inc(v_set, 1)
                dve.memset(vm_pair[k][:], 0.0).then_inc(v_set, 1)
            for t in range(GT):
                max_a(0, t)
            for t in range(GT):
                normalise_a(0, t)
            for gg in range(NB * G):
                b, g = gg // G, gg % G
                if gg == PREP_1[0]:
                    prep_x(1)
                if gg == PREP_1[2]:
                    prep_k(1, 7)
                if gg == PREP_1[3]:
                    prep_v(1, 7)
                if gg == WO_0:
                    residual_a(0)
                if gg == LN_0:
                    ln_begin(0, row_tiles(z, 0))
                if gg == APPLY_0:
                    ln_apply(0, row_tiles(z, 0), x1[0])
                if gg == LN_1:
                    ln_begin(1, x1[0])
                if gg == APPLY_1:
                    ln_apply(1, x1[0], x1n)
                if gg == PIECES_0[MEM]:
                    piece(0, 0, MEM)
                if gg in (PIECES_0[Q] + 1, PIECES_0[K] + 1):
                    piece(0, 0, PIECES_0.index(gg - 1))
                if gg + 1 < NB * G:
                    max_a(gg + 1, 0)
                else:
                    max_b(0, 0)
                for t in range(GT):
                    if gg + 1 < NB * G and t < GT - 1:
                        max_a(gg + 1, t + 1)
                    if t == 0 and gg > 0:
                        take_out(gg - 1)
                    n = b * NTR + TR0[g] + t
                    if t < chunks(g) and n % 2 == 0:
                        rows_n = min(P, GI * (g + 1) - P * t)
                        dve.wait_ge(pe_tra, n + 1)
                        dve.tensor_copy(probT_a[0:rows_n, t, :], bank[0:rows_n, 4, :]).then_inc(v_eva, 1)
                    if gg + 1 < NB * G:
                        normalise_a(gg + 1, t)
                    elif t == 0:
                        max_b(0, 1)
                    elif t < 3:
                        recip_b(0, t - 1, 0)
            take_out(NB * G - 1)

            def unit(pg, k, it, slot=None):
                u = pg * 4 + it
                last = slot == NB * NU - 1
                projects = slot is None or slot < NB * NU - T
                if not last:
                    max_b(u + 1, 0)
                dve.wait_ge(pe_trb, u * 2 + 1)
                dve.tensor_copy(probT_b[0][:], bank[:, 4, :].rearrange("p (c n) -> p c n", n=P)).then_inc(v_evb, 1)
                if slot == 0:
                    residual_a(1)
                if slot == NU:
                    residual_b(0)
                dve.wait_ge(pe_trb, u * 2 + 2)
                dve.tensor_copy(probTm[:], bank[0:2 * M, 6, P:2 * P]).then_inc(v_evm, 1)
                if projects and it == 0:
                    piece(pg + 1, 1 - k, MEM, 6)
                if not last:
                    max_b(u + 1, 1)
                if projects and it == 2:
                    piece(pg + 1, 1 - k, K)
                if not last:
                    recip_b(u + 1, 0, 1 - it % 2)
                    recip_b(u + 1, 1, 1 - it % 2)
                if projects and it == 1:
                    piece(pg + 1, 1 - k, Q)
                if slot == 0:
                    ln_begin(2, row_tiles(z, 1))
                if slot == 1:
                    ln_apply(2, row_tiles(z, 1), x1[1])
                    ln_begin(3, x1[1])
                if slot == 2:
                    ln_apply(3, x1[1], x1n)
                if slot == NU:
                    ln_begin(4, row_tiles(z, 0))
                if slot == NU + 2:
                    ln_apply(4, row_tiles(z, 0), row_tiles(x2, 0))

            for b in range(NB):
                for it in range(T):
                    unit(b * NP, 0, it, b * NU + it)
                with dve.Fori(0, NP // 2 - 1) as r:
                    for k in (1, 0):
                        for it in range(T):
                            unit(r * 2 + (b * NP + 2 - k), k, it)
                for it in range(T):
                    unit(b * NP + NP - 1, 1, it, b * NU + NU - T + it)

            residual_b(1)
            ln_begin(5, row_tiles(z, 1))
            ln_apply(5, row_tiles(z, 1), row_tiles(x2, 1))

            def step(ins, n):
                ins.then_inc(v_m, 1)
                dve.wait_ge(v_m, n)

            def over_experts(col):
                return tok[:, col, :].unsqueeze(2).broadcast_to([P, TT, NE])

            dve.wait_ge(pe_m, 4)
            logits = bank[:, 4, 0:TT * NE].rearrange("p (t e) -> p t e", e=NE)
            step(dve.tensor_reduce(tok[:, 0, :], logits, AX.X, ALU.max), 1)
            step(dve.tensor_tensor(lg[:], logits, over_experts(0), ALU.subtract), 2)
            dve.wait_ge(a_m, 3)
            step(dve.tensor_reduce(tok[:, 1, :], ex[:], AX.X, ALU.max), 3)
            step(dve.tensor_tensor(cand[:], ex[:], over_experts(1), ALU.is_ge), 4)
            dve.wait_ge(g_const, 17)
            step(dve.tensor_tensor(cand[:], cand[:], rank[:].unsqueeze(1).broadcast_to([P, TT, NE]), ALU.mult), 5)
            step(dve.tensor_reduce(tok[:, 4, :], cand[:], AX.X, ALU.max), 6)
            step(dve.tensor_tensor(chosen[:], cand[:], over_experts(4), ALU.is_equal), 7)
            step(dve.tensor_copy(chosen_bf[:], chosen[:]), 8)
            dve.tensor_reduce(tok[:, 2, :], ex[:], AX.X, ALU.add).then_inc(v_gate, 1)
            dve.wait_ge(v_gate, 1)
            dve.reciprocal(tok[:, 2, :], tok[:, 2, :]).then_inc(v_gate, 1)
            dve.wait_ge(v_gate, 2)
            dve.tensor_tensor(tok[:, 3, :], tok[:, 1, :], tok[:, 2, :], ALU.mult).then_inc(v_gate, 1)
            dve.wait_ge(v_gate, 3)
            dve.wait_ge(pe_m, 5)
            places = bank[:, 5, 0:TT * NE].rearrange("p (t e) -> p t e", e=NE)
            step(dve.scalar_tensor_tensor(out=coef[:], in0=places, scalar=float(CAP), in1=chosen[:],
                                          op0=ALU.is_lt, op1=ALU.mult), 9)
            step(dve.tensor_tensor(coef[:], coef[:], over_experts(3), ALU.mult), 10)

            def accumulate(t, e):
                if e == 0:
                    dve.wait_ge(pe_y, t + 1)
                else:
                    dve.wait_ge(v_acc, 4 * t + e)
                y = bank[:, EXPERT_BANKS[t % 3], e * E:(e + 1) * E]
                dve.scalar_tensor_tensor(out=z[:, t, :], in0=y, scalar=coef[:, t, e:e + 1],
                                         in1=(z if e else x2)[:, t, :], op0=ALU.mult,
                                         op1=ALU.add).then_inc(v_acc, 1)

            def finish(t, n):
                if n == 0:
                    dve.wait_ge(g_sum, 2 * (t + 1))
                    dve.wait_ge(v_acc, 4 * (t + 1))
                    dve.tensor_tensor(z[:, t, :], z[:, t, :], parts[t % 3][:, 0, :], ALU.add).then_inc(v_fin, 1)
                if n == 1:
                    dve.wait_ge(pe_m, 7)
                    dve.wait_ge(v_fin, 2 * t + 1)
                    dve.tensor_tensor(z[:, t, :], bank[:, 4 + t // 4, (t % 4) * P:(t % 4 + 1) * P], z[:, t, :],
                                      ALU.add).then_inc(v_fin, 1)
                if n == 2:
                    dve.wait_ge(v_fin, 2 * t + 2)
                    dve.bn_stats(stats[:, t, :], z[:, t, :]).then_inc(v_lnf, 1)

            def last_ln_begin(b):
                for t in range(b * T, (b + 1) * T):
                    dve.wait_ge(v_lnf, t + 1)
                    dve.bn_aggr(moments[:, t, :], stats[:, t, :]).then_inc(v_lnm, 1)
                dve.wait_ge(v_lnm, LN_MORE * b + T)
                dve.tensor_scalar(var_eps[:, b * T:(b + 1) * T], moments[:, b * T:(b + 1) * T, 1], EPS, None,
                                  ALU.add).then_inc(v_lnm, 1)

            def last_ln_apply(b):
                dve.wait_ge(g_powf, b + 1)
                for t in range(b * T, (b + 1) * T):
                    dve.tensor_scalar(y_out[:, t, :], z[:, t, :], moments[:, t, 0:1], rstd[:, t:t + 1],
                                      ALU.subtract, ALU.mult).then_inc(v_lnm, 1)

            for t in range(TT + 1):
                for e in range(4):
                    if t < TT:
                        accumulate(t, e)
                    if t > 0 and e < 3:
                        finish(t - 1, e)
                if t == T:
                    last_ln_begin(0)
                if t == TT - 1:
                    last_ln_apply(0)
            last_ln_begin(1)
            last_ln_apply(1)


_INS = ['x', 'ctx_1024', 'L0_attn_Wq', 'L0_attn_bq', 'L0_attn_Wk', 'L0_attn_bk', 'L0_attn_Wv', 'L0_attn_bv',
        'L0_attn_Wo', 'L0_attn_bo', 'L0_attn_rel_key', 'L0_xattn_ln_g', 'L0_xattn_ln_b', 'L0_xattn_Wq',
        'L0_xattn_Wkv', 'L0_xattn_Wm', 'L0_xattn_Wo', 'L0_xattn_bo', 'L0_ffn_wg', 'L0_ffn_W', 'L0_ffn_b']


def kernel(**inputs):
    import numpy as np
    import concourse.bacc as bacc
    from concourse.bass_utils import run_bass_kernel_spmd

    nc = bacc.Bacc("TRN2", target_bir_lowering=False, num_devices=1)
    arrays, args = {}, []
    for name in _INS:
        a = np.ascontiguousarray(inputs[name])
        arrays[f"in_{name}"] = a
        args.append(nc.dram_tensor(f"in_{name}", a.shape, mybir.dt.from_np(a.dtype), kind="ExternalInput").ap())
    out = nc.dram_tensor("out_x", (NB, S, E), F32, kind="ExternalOutput").ap()
    decoder_layer(nc, *args, out)
    return run_bass_kernel_spmd(nc, [arrays], core_ids=[0]).results[0]["out_x"]
```

```python
from contextlib import ExitStack

import concourse.bass as bass
from concourse import mybir
from concourse.alu_op_type import AluOpType as ALU

F32 = mybir.dt.float32
F32R = mybir.dt.float32r
BF16 = mybir.dt.bfloat16
ACT = mybir.ActivationFunctionType
AX = mybir.AxisListType

P = 128
NB, S, E = 2, 512, 128
T = S // P
EPS = 1e-5
NEG = -1e30

H, HD, REL = 16, 8, 256
QI = P // H
GI = 32
GT = GI // QI
G = S // GI
WIN = S - QI
TW = WIN + GI
SCALE_A = HD ** -0.5


def chunks(g):
    return -(-GI * (g + 1) // P)


TR0 = [sum(chunks(k) for k in range(g)) for g in range(G + 1)]
NTR = TR0[G]
assert NTR % 4 == 0

XD, M = 64, 32
NP = 8
B_LOOPS = 2
KEYS = S + M
KH = KEYS // 2
NU = NP * T
SCALE_B = XD ** -0.5

NE, CAP = 8, NB * S // 8
EXPERT_BANKS = (2, 0, 6)
X2T_BANKS = (0, 5)
TT = NB * T

PREP_1 = (1, 3, 5, 7)
X_PLUS_BO = (10, 14)
SETUP = (9, 11, 13)
WO_0, LN_0, APPLY_0, LN_1, APPLY_1, XN_0 = 17, 18, 20, 21, 23, 24
PIECES_0 = (25, 26, 27, 28)
Q_1 = 29
SPLIT_XN = (1, 20)
FIRST_SPLIT = 2
LNS = ((0, "attention"), (0, "inner"), (1, "attention"), (1, "inner"), (0, "memories"), (1, "memories"))
LN_MORE = 2 * T + 1
LN_BEGIN, LN = 2 * T + 1, 3 * T + 1
N_LOADS_A, N_LOADS_B = 5, 11
OWN = (slice(0, XD), slice(XD, 2 * XD))
OTHER = OWN[::-1]
TOKENS = (slice(0, S), slice(M, KEYS))
MEMORIES = (slice(S, KEYS), slice(0, M))
Q, MEM, K, V = range(4)
Q_REP_PARTS = ((0, slice(0, P)), (0, slice(P, S)), (1, slice(0, S)))
A_PJ, V_PJ, G_PJ = 7, 8, 4
A_Q, A_K = 3, 6
V_MEM = 6


def decoder_layer(nc, x, ctx, wq, bq, wk, bk, wv, bv, wo, bo, rel, ln_g, ln_b, xwq, xwkv, xwm, xwo, xbo,
                  wg, we, be, out):
    with ExitStack() as stack:
        def sb(name, shape, dt=F32):
            return stack.enter_context(nc.sbuf_tensor(name, shape, dt))

        def sem(name):
            return stack.enter_context(nc.semaphore(name))

        ident = sb("ident", [P, P])
        ones_row = sb("ones_row", [1, P])
        ones_bf = sb("ones_bf", [P, P], BF16)
        before = sb("before", [P, P], BF16)
        head_mask = sb("head_mask", [P, H])
        quad_mask = sb("quad_mask", [P, 4])
        power = sb("power", [P, TT])
        rank = sb("rank", [P, NE])
        wqkv = sb("wqkv", [P, 3, E])
        wo_sb = sb("wo_sb", [P, E])
        bcols = sb("bcols", [P, 6])
        rel0_row = sb("rel0_row", [1, H, HD])
        bias_rows = sb("bias_rows", [P, 3, E])
        xbo_row = sb("xbo_row", [1, E])
        rel_sb = sb("rel_sb", [P, REL // P, HD])
        rel_ext = sb("rel_ext", [HD, TW + QI])
        minus_rel0 = sb("minus_rel0", [HD, 1])
        toep = sb("toep", [P, TW])
        xwo_sb = sb("xwo_sb", [P, NP, E])
        ctx_sb = sb("ctx_sb", [NB * M, E])
        ctxT = sb("ctxT", [P, NB * M])
        wg_sb = sb("wg_sb", [P, NE])
        we_sb = sb("we_sb", [P, NE, E])
        weT = sb("weT", [P, NE, E])
        be_sb = sb("be_sb", [NE, E])
        x_sb = [sb(f"x_sb{b}", [P, T, E]) for b in range(NB)]
        xT = sb("xT", [P, S])
        qT = [sb(f"qT{b}", [P, S]) for b in range(NB)]
        kT = [sb(f"kT{b}", [P, S]) for b in range(NB)]
        v_sb = [sb(f"v_sb{b}", [P, T, E]) for b in range(NB)]
        q_rep = sb("q_rep", [NB * QI * HD, H, S])
        q_heads = [sb(f"q_heads{k}", [P, GI, H]) for k in range(2)]
        q_pos = [sb(f"q_pos{k}", [P, GI, H]) for k in range(2)]
        prob_a = [sb(f"prob_a{k}", [P, GT, S]) for k in range(2)]
        stat_a = sb("stat_a", [P, 3, 2, GT])
        probT_a = sb("probT_a", [P, T, GT * P])
        o_masked = sb("o_masked", [P, GI, 4])
        outT_a = [sb(f"outT_a{b}", [P, S]) for b in range(NB)]
        def f32r_view(n):
            return q_rep[:, n, :].bitcast(F32R)

        xn_high, xn_low = [f32r_view(2 * b) for b in range(NB)], [f32r_view(2 * b + 1) for b in range(NB)]
        w_high, w_low = [[f32r_view(4 + k)[:, n * 2 * P:(n + 1) * 2 * P].rearrange("p (j n) -> p j n", n=P)
                          for k in range(2)] for n in range(2)]
        z = sb("z", [P, TT, E])
        stats = sb("stats", [P, TT, 6])
        moments = sb("moments", [P, TT, 2])
        var_eps = sb("var_eps", [P, TT])
        rstd = sb("rstd", [P, TT])
        x1 = [sb(f"x1_{b}", [P, T, E]) for b in range(NB)]
        x1n = sb("x1n", [P, T, E])
        x2 = sb("x2", [P, TT, E])
        w_pair = [sb(f"w_pair{k}", [P, 4, P]) for k in range(2)]
        xnT = [sb(f"xnT{b}", [P, S]) for b in range(NB)]
        q_high = [sb(f"q_high{k}", [P, 2, S], F32R) for k in range(2)]
        q_low = [sb(f"q_low{k}", [P, 2, S], F32R) for k in range(2)]
        k_split = [sb(f"k_split{k}", [P, 2, KEYS], F32R) for k in range(2)]
        q_raw, k_raw = sb("q_raw", [P, S]), sb("k_raw", [P, S])
        v_pair = [sb(f"v_pair{k}", [P, T, P]) for k in range(2)]
        vm_pair = [sb(f"vm_pair{k}", [2 * M, P]) for k in range(2)]
        prob_b = [sb(f"prob_b{i}", [P, 2, KEYS]) for i in range(2)]
        stat_b = sb("stat_b", [P, 3, 2])
        probT_b = [sb(f"probT_b{h}", [P, T, P]) for h in range(2)]
        probTm = sb("probTm", [2 * M, P])
        outT_b = sb("outT_b", [P, NP, S])
        x2T = sb("x2T", [P, TT * P])
        lg = sb("lg", [P, TT, NE])
        ex = sb("ex", [P, TT, NE])
        cand = sb("cand", [P, TT, NE])
        chosen = sb("chosen", [P, TT, NE])
        chosen_bf = sb("chosen_bf", [P, TT, NE], BF16)
        coef = sb("coef", [P, TT, NE])
        tok = sb("tok", [P, 5, TT])
        coefT = sb("coefT", [NE, TT * P])
        parts = [probT_a[:, k, :].rearrange("p (e n) -> p e n", n=E) for k in range(3)]
        y_out = prob_a[0][:].rearrange("p t n -> p (t n)")[:, 0:TT * E].rearrange("p (t e) -> p t e", e=E)

        q_scratch = nc.dram_tensor("q_scratch", (NB, P, S), F32, kind="Internal").ap()

        bank = stack.enter_context(nc.psum_tensor("bank", [P, 8, 512], F32))

        ld_x, ld_q, ld_rel, ld_a, ld_b = [sem("ld_x0"), sem("ld_x1")], sem("ld_q"), sem("ld_rel"), sem("ld_a"), sem("ld_b")
        ld_pair = [sem("ld_pair0"), sem("ld_pair1")]
        sc_w, sc_r = [[sem(f"{name}{n}") for n in range(len(Q_REP_PARTS))] for name in ("scratch_written", "q_rep_loaded")]
        g_const, v_set, v_bias, pe_set, a_set = sem("g_const"), sem("v_set"), sem("v_bias"), sem("pe_set"), sem("a_set")
        ld_toep = sem("toeplitz_loaded")
        pe_prep, v_prep, a_prep = sem("pe_prep"), sem("v_prep"), sem("a_prep")
        g_build = sem("g_build")
        v_xs, g_xs, v_ws, g_ws = sem("v_xn_high"), sem("g_xn_low"), sem("v_w_high"), sem("g_w_low")
        g_bias = sem("g_bias")
        pe_sa, v_maxa, a_expa, v_rca, v_na = sem("pe_scores_a"), sem("v_max_a"), sem("a_exp_a"), sem("v_recip_a"), sem("v_norm_a")
        pe_tra, v_eva, a_eva, pe_pva, v_oa = sem("pe_transposed_a"), sem("v_evac_a"), sem("a_evac_a"), sem("pe_pv_a"), sem("v_out_a")
        pe_wo, v_za, v_zb, v_ln, g_pow = sem("pe_wo"), sem("v_resid_a"), sem("v_resid_b"), sem("v_ln"), sem("g_pow")
        pe_xn, a_xn = sem("pe_xn"), sem("a_xn")
        pe_pj, a_pj, v_pj, g_pj = sem("pe_proj"), sem("a_proj"), sem("v_proj"), sem("g_proj")
        pe_sb, v_maxb, a_expb, v_rcb, v_nb, g_nb = sem("pe_scores_b"), sem("v_max_b"), sem("a_exp_b"), sem("v_recip_b"), sem("v_norm_b"), sem("g_norm_b")
        pe_trb, v_evb, v_evm, a_evb, pe_pvb, a_ob = sem("pe_transposed_b"), sem("v_evac_b"), sem("v_evac_mem"), sem("a_evac_b"), sem("pe_pv_b"), sem("a_out_b")
        pe_wob = sem("pe_wo_b")
        pe_m, v_m, a_m = sem("pe_moe"), sem("v_moe"), sem("a_moe")
        pe_y, v_gate, v_acc, v_fin, v_lnf = sem("pe_expert"), sem("v_gate"), sem("v_acc"), sem("v_finish"), sem("v_stats_final")
        v_lnm, a_part, g_sum = sem("v_ln_final"), sem("a_part"), sem("g_sum")
        g_powf, st_out = sem("g_pow_final"), sem("stored")

        x_rows = x.rearrange("b (t p) e -> b p t e", p=P)
        out_rows = out.rearrange("b (t p) e -> p (b t) e", p=P)

        passed = {name: sem(f"passed_{name}") for name in ("pool", "pe", "dve")}

        def stand_alone(eng, name):
            eng.sem_inc(passed[name])

        block = stack.enter_context(nc.Block())

        @block.sync
        def _(sp):
            sp.dma_start(x_sb[0][:], x_rows[0]).then_inc(ld_x[0], 16)
            sp.dma_start(wqkv[:, 0, :], wq).then_inc(ld_q, 16)
            sp.dma_start(bcols[:, 0:1], bq.rearrange("(p a) -> p a", a=1)).then_inc(ld_q, 16)
            sp.dma_start(wqkv[:, 1, :], wk).then_inc(ld_a, 16)
            sp.dma_start(wqkv[:, 2, :], wv).then_inc(ld_a, 16)
            sp.dma_start(bcols[:, 1:2], bk.rearrange("(p a) -> p a", a=1)).then_inc(ld_a, 16)
            sp.dma_start(rel0_row[:], rel[0:1, :].unsqueeze(1).broadcast_to([1, H, HD])).then_inc(ld_a, 16)
            sp.dma_start(bias_rows[:, 0, :], bv.rearrange("(a n) -> a n", a=1).broadcast_to([P, E])).then_inc(ld_a, 16)
            for b in range(NB):
                sp.wait_ge(a_prep, b + 1)
                for n, (row, part) in enumerate(Q_REP_PARTS):
                    if row == b:
                        sp.dma_start(q_scratch[b, :, part], qT[b][:, part]).then_inc(sc_w[n], 16)
                for n, (row, part) in enumerate(Q_REP_PARTS):
                    if row == b:
                        sp.wait_ge(sc_w[n], 16)
                        for i in range(b * QI, (b + 1) * QI):
                            sp.dma_start(q_rep[HD * i:HD * (i + 1), :, part],
                                         q_scratch[b, :, part].rearrange("(h d) i -> d h i", d=HD)).then_inc(sc_r[n], 16)
                if b == 0:
                    sp.dma_start(x_sb[1][:], x_rows[1]).then_inc(ld_x[1], 16)
                    sp.dma_start(wo_sb[:], wo).then_inc(ld_b, 16)
                    sp.dma_start(xwo_sb[:], xwo.rearrange("(c p) n -> p c n", p=P)).then_inc(ld_b, 16)
                    sp.dma_start(xbo_row[:], xbo.rearrange("(a n) -> a n", a=1)).then_inc(ld_b, 16)
                    for n, row in ((1, bo), (2, xbo)):
                        sp.dma_start(bias_rows[:, n, :],
                                     row.rearrange("(a n) -> a n", a=1).broadcast_to([P, E])).then_inc(ld_b, 16)
                    sp.dma_start(bcols[:, 2:3], ln_g.rearrange("(p a) -> p a", a=1)).then_inc(ld_b, 16)
                    sp.dma_start(bcols[:, 3:4], ln_b.rearrange("(p a) -> p a", a=1)).then_inc(ld_b, 16)
                    sp.dma_start(ctx_sb[:], ctx.rearrange("b m e -> (b m) e")).then_inc(ld_b, 16)
                    sp.dma_start(wg_sb[:], wg).then_inc(ld_b, 16)
                    sp.dma_start(we_sb[:], we.rearrange("e f h -> f e h")).then_inc(ld_b, 16)
                    sp.dma_start(be_sb[:], be).then_inc(ld_b, 16)

            def load_pair(p, k):
                for j, src in enumerate((xwq[:, bass.ds(p * P, P)], xwkv[:, bass.ds(p * P, P)],
                                         xwkv[:, bass.ds(p * P + NP * P, P)], xwm[:, bass.ds(p * P, P)])):
                    sp.dma_start(w_pair[k][:, j, :], src).then_inc(ld_pair[k], 16)

            load_pair(0, 0)
            load_pair(1, 1)
            for b in range(NB):
                with sp.Fori(1 - b, NP // 2) as r:
                    for k in range(2):
                        sp.wait_ge(pe_pj, r * 8 + (b * 4 * NP + 4 * (k - 1)))
                        load_pair(r * 2 + k, k)
            for n in range(NB):
                sp.wait_ge(v_lnm, LN_MORE * (n + 1))
                sp.dma_start(out_rows[:, T * n:T * (n + 1), :], y_out[:, T * n:T * (n + 1), :]).then_inc(st_out, 16)
            sp.wait_ge(st_out, 16 * NB)

        @block.gpsimd
        def _(pool):
            def masked(out, base, mult, pattern, op, fill, n):
                pool.wait_ge(g_const, n)
                pool.affine_select(out=out, in_=out, compare_op=op, fill=fill, base=base, pattern=pattern,
                                   channel_multiplier=mult).then_inc(g_const, 1)

            pool.memset(ident[:], 0.0).then_inc(g_const, 1)
            masked(ident[:], 0, 1, [[-1, P]], ALU.not_equal, 1.0, 1)
            pool.memset(head_mask[:], 1.0).then_inc(g_const, 1)
            masked(head_mask[:], 0, 1, [[-HD, H]], ALU.is_ge, 0.0, 3)
            masked(head_mask[:], HD - 1, -1, [[HD, H]], ALU.is_ge, 0.0, 4)
            pool.memset(toep[:], 0.0).then_inc(g_const, 1)
            masked(toep[:], WIN - QI * HD, 1, [[-1, TW]], ALU.is_ge, NEG, 6)
            for k in range(2):
                pool.memset(q_pos[k][:], 0.0).then_inc(g_const, 1)
            pool.memset(ones_row[:], 1.0).then_inc(g_const, 1)
            for k in range(2):
                masked(q_pos[k][:].rearrange("p (t i) h -> p t i h", i=QI), -QI * HD, 1,
                       [[0, GT], [-1, QI], [0, H]], ALU.not_equal, 1.0, 9)
            pool.memset(power[:], -0.5).then_inc(g_const, 1)
            pool.memset(ones_bf[:], 1.0).then_inc(g_const, 1)
            pool.memset(before[:], 1.0).then_inc(g_const, 1)
            masked(before[:], -1, -1, [[1, P]], ALU.is_ge, 0.0, 15)
            pool.iota(rank[:], [[-1, NE]], base=NE, channel_multiplier=0, allow_small_or_imprecise_dtypes=True).then_inc(g_const, 1)

            def build(gg):
                k, b, g = gg % 2, gg // G, gg % G
                if g == 0:
                    pool.wait_ge(a_prep, b + 1)
                if gg >= 2:
                    pool.wait_ge(pe_sa, GT * (gg - 1))
                cols = qT[b][:, GI * g:GI * (g + 1)].unsqueeze(2).broadcast_to([P, GI, H])
                pool.tensor_tensor(q_heads[k][:], cols, head_mask[:].unsqueeze(1).broadcast_to([P, GI, H]),
                                   ALU.mult).then_inc(g_build, 1)
                for n, (row, part) in enumerate(Q_REP_PARTS):
                    if row == b and part.start == GI * g:
                        pool.wait_ge(sc_r[n], 16 * QI)
                if b > 0:
                    pool.wait_ge(g_build, 2 * gg + 1)
                n = QI * HD
                part = slice(n * b, n * (b + 1))
                rep = q_rep[part, :, GI * g:GI * (g + 1)].rearrange("p h (t i) -> p t i h", i=QI)
                pick = head_mask[part, QI * b:QI * (b + 1)].unsqueeze(1).unsqueeze(3).broadcast_to([n, GT, QI, H])
                pool.tensor_tensor(q_pos[k][0:n].rearrange("p (t i) h -> p t i h", i=QI), rep, pick,
                                   ALU.mult).then_inc(g_build, 1)
                if b > 0:
                    pool.wait_ge(g_build, 2 * gg + 2)

            def rsqrt(n):
                pool.wait_ge(v_ln, LN * n + LN_BEGIN)
                pool.tensor_tensor(rstd[:, 0:T], var_eps[:, 0:T], power[:, 0:T], ALU.pow).then_inc(g_pow, 1)
                pool.wait_ge(g_pow, n + 1)

            def normalise(u, i):
                pool.wait_ge(v_rcb, u * 2 + 1)
                stand_alone(pool, "pool")
                row = prob_b[i][:, 0, :]
                pool.tensor_scalar(row, row, stat_b[:, 2, 0:1], 1.0, ALU.mult,
                                   ALU.mult).then_inc(g_nb, 1)

            def split(pg, k, j):
                pool.wait_ge(a_pj, pg * A_PJ + (A_Q if j == Q else A_K))
                for h in range(2):
                    if j == K or h == 1:
                        pool.wait_ge(g_pj, pg * G_PJ + (j + h))
                    stand_alone(pool, "pool")
                    if j == Q:
                        out, raw, high = q_low[k][OWN[h], h, :], q_raw, q_high[k][OWN[h], h, :]
                    else:
                        out, raw, high = k_split[k][OTHER[h], h, TOKENS[h]], k_raw, k_split[k][OWN[h], h, TOKENS[h]]
                    pool.tensor_tensor(out, raw[OWN[h], :], high.bitcast(F32), ALU.subtract).then_inc(g_pj, 1)
                pool.wait_ge(g_pj, pg * G_PJ + (j + 2))

            def add_bias(tile, n):
                pool.tensor_tensor(tile[:], tile[:], bias_rows[:, n:n + 1, :].broadcast_to([P, T, E]),
                                   ALU.add).then_inc(g_bias, 1)

            for gg in range(NB * G):
                if gg in X_PLUS_BO:
                    b = X_PLUS_BO.index(gg)
                    pool.wait_ge(pe_prep, 4 * b + 1)
                    pool.wait_ge(ld_b, 16 * N_LOADS_B)
                    add_bias(x_sb[b], 1)
                if gg == PIECES_0[Q] + 3:
                    split(0, 0, Q)
                if gg == PIECES_0[K] + 3:
                    split(0, 0, K)
                if gg == LN_0 + 3:
                    rsqrt(0)
                if gg == LN_1 + 3:
                    rsqrt(1)
                build(gg)
            def unit(pg, k, it, slot=None):
                u = pg * 4 + it
                if slot != NB * NU - 1:
                    normalise(u + 1, 1 - it % 2)
                if slot in SPLIT_XN:
                    b = SPLIT_XN.index(slot)
                    pool.wait_ge(v_xs, b + 1)
                    pool.tensor_tensor(xn_low[b], xnT[b][:], xn_high[b].bitcast(F32), ALU.subtract).then_inc(g_xs, 1)
                    pool.wait_ge(g_xs, b + 1)
                if it == 2 and (slot is None or slot < NB * NU - 2 * T):
                    pool.wait_ge(v_ws, pg + 1)
                    stand_alone(pool, "pool")
                    pool.tensor_tensor(w_low[k], w_pair[k][:, 0:2, :], w_high[k].bitcast(F32),
                                       ALU.subtract).then_inc(g_ws, 1)
                    pool.wait_ge(g_ws, pg + 1)
                if it < 2 and (slot is None or slot < NB * NU - T):
                    pool.wait_ge(g_nb, u + 2)
                    split(pg + 1, 1 - k, (Q, K)[it])
                if slot in (0, 1):
                    rsqrt(2 + slot)
                if slot == NU:
                    rsqrt(4)

            pool.wait_ge(v_ln, 2 * LN)
            add_bias(x1[0], 2)
            pool.wait_ge(g_bias, 3)
            normalise(0, 0)
            for b in range(NB):
                for it in range(T):
                    unit(b * NP, 0, it, b * NU + it)
                with pool.Fori(0, B_LOOPS) as r:
                    for k in (1, 0):
                        for it in range(T):
                            unit(r * 2 + (b * NP + 2 - k), k, it)
                for p in range(2 * B_LOOPS + 1, NP):
                    for it in range(T):
                        unit(b * NP + p, p % 2, it, b * NU + p * T + it)
            rsqrt(5)
            for t in range(TT):
                part = parts[t % 3]
                pool.wait_ge(a_part, 4 * (t + 1))
                pool.tensor_tensor(part[:, 0:2, :], part[:, 0:2, :], part[:, 2:4, :], ALU.add).then_inc(g_sum, 1)
                pool.wait_ge(g_sum, 2 * t + 1)
                pool.tensor_tensor(part[:, 0, :], part[:, 0, :], part[:, 1, :], ALU.add).then_inc(g_sum, 1)
                if t == 5 or t == TT - 1:
                    b = int(t == TT - 1)
                    pool.wait_ge(v_lnm, LN_MORE * b + T + 1)
                    pool.tensor_tensor(rstd[:, T * b:T * (b + 1)], var_eps[:, T * b:T * (b + 1)],
                                       power[:, 0:T], ALU.pow).then_inc(g_powf, 1)

        @block.scalar
        def _(act):
            def copy(out, in_, done):
                act.activation(out, in_, ACT.Copy).then_inc(done, 1)

            act.dma_start(rel_sb[:], rel.rearrange("(c p) d -> p c d", p=P)).then_inc(ld_rel, 16)

            act.wait_ge(pe_set, 1)
            r_cols = bank[0:HD, 0, 0:REL]
            act.activation(minus_rel0[:], r_cols[:, 0:1], ACT.Copy, scale=-1.0).then_inc(a_set, 1)
            act.wait_ge(a_set, 1)

            def less_rel0(out, in_):
                act.activation(out, in_, ACT.Identity, bias=minus_rel0[:], scale=1.0).then_inc(a_set, 1)

            less_rel0(rel_ext[:, REL:2 * REL], r_cols)
            less_rel0(rel_ext[:, 0:REL], r_cols[:, 0:1].broadcast_to([HD, REL]))
            rest = TW + QI - 2 * REL
            less_rel0(rel_ext[:, 2 * REL:], r_cols[:, REL - 1:REL].broadcast_to([HD, rest]))
            def prep_q(b, n):
                act.wait_ge(pe_prep, 4 * b + 2)
                act.activation(qT[b][:], bank[:, n, :], ACT.Identity, bias=bcols[:, 4:5],
                               scale=SCALE_A).then_inc(a_prep, 1)

            def xn_evac(b):
                act.wait_ge(pe_xn, b + 1)
                act.activation(xnT[b][:], bank[:, 7, :], ACT.Identity, bias=bcols[:, 3:4],
                               scale=bcols[:, 2:3]).then_inc(a_xn, 1)

            def exp_a(gg, t):
                act.wait_ge(v_maxa, GT * gg + t + 1)
                n = GI * (gg % G + 1)
                act.activation(prob_a[gg % 2][:, t, 0:n], bank[:, t, 0:n], ACT.Exp,
                               bias=stat_a[:, 0, gg % 2, t:t + 1], scale=1.0,
                               accum_out=stat_a[:, 1, gg % 2, t:t + 1]).then_inc(a_expa, 1)

            def piece(pg, k, j):
                act.wait_ge(pe_pj, pg * 4 + (j + 1))
                if j == Q:
                    act.activation(q_raw[:], bank[:, 7, :], ACT.Copy, scale=SCALE_B).then_inc(a_pj, 1)
                    for h in range(2):
                        act.activation(q_high[k][OWN[h], h, :], bank[OWN[h], 7, :], ACT.Copy,
                                       scale=SCALE_B).then_inc(a_pj, 1)
                if j == K:
                    copy(k_raw[:], bank[:, 7, :], a_pj)
                    for h in range(2):
                        copy(k_split[k][OWN[h], h, TOKENS[h]], bank[OWN[h], 7, :], a_pj)
                if j == V:
                    copy(v_pair[k][:], bank[:, 7, :].rearrange("p (t n) -> p t n", n=P), a_pj)

            def exp_b(u, h, i):
                act.wait_ge(v_maxb, u * 2 + (h + 1))
                act.activation(prob_b[i][:, h, :].rearrange("p (c n) -> p c n", c=2), bank[:, 2 * h:2 * h + 2, 0:KH],
                               ACT.Exp, bias=stat_b[:, 0, h:h + 1], scale=1.0,
                               accum_out=stat_b[:, 1, h:h + 1]).then_inc(a_expb, 1)

            act.wait_ge(v_set, 1)
            prep_q(0, 4)
            act.wait_ge(a_set, 4)
            act.wait_ge(g_const, 7)
            for i in range(QI):
                act.dma_start(toep[HD * i:HD * (i + 1), :],
                             rel_ext[:, QI - 1 - i:QI - 1 - i + TW]).then_inc(ld_toep, 16)
            for t in range(GT):
                exp_a(0, t)
            for gg in range(NB * G):
                if gg == PREP_1[1]:
                    prep_q(1, 7)
                if gg in SETUP:
                    n = SETUP.index(gg)
                    act.wait_ge(pe_set, n + 2)
                    if n < 2:
                        copy(weT[:, 4 * n:4 * n + 4, :], bank[:, 7, :].rearrange("p (e f) -> p e f", f=E), a_set)
                    else:
                        copy(ctxT[:], bank[:, 7, 0:NB * M], a_set)
                if gg == XN_0:
                    act.wait_ge(ld_b, 16 * N_LOADS_B)
                    xn_evac(0)
                if gg in PIECES_0 and gg != PIECES_0[MEM]:
                    piece(0, 0, PIECES_0.index(gg))
                if gg == Q_1:
                    act.wait_ge(g_pj, 2)
                    act.wait_ge(v_pj, V_PJ)
                    piece(1, 1, Q)
                if gg + 1 < NB * G:
                    exp_a(gg + 1, 0)
                for t in range(GT):
                    if gg + 1 < NB * G and t < GT - 1:
                        exp_a(gg + 1, t + 1)
                    if gg == NB * G - 1 and t < 2:
                        exp_b(0, t, 0)
                    n = gg // G * NTR + TR0[gg % G] + t
                    if t < chunks(gg % G) and n % 2 == 1:
                        rows_n = min(P, GI * (gg % G + 1) - P * t)
                        act.wait_ge(pe_tra, n + 1)
                        copy(probT_a[0:rows_n, t, :], bank[0:rows_n, 5, :], a_eva)

            def unit(pg, k, it, slot=None):
                u = pg * 4 + it
                last = slot == NB * NU - 1
                act.wait_ge(pe_trb, u * 2 + 2)
                copy(probT_b[1][:], bank[:, 5, :].rearrange("p (c n) -> p c n", n=P), a_evb)
                if not last:
                    exp_b(u + 1, 0, 1 - it % 2)
                    exp_b(u + 1, 1, 1 - it % 2)
                if slot == 3:
                    xn_evac(1)
                act.wait_ge(pe_pvb, u + 1)
                p = slot // T % NP if slot is not None else pg - pg_row[0]
                copy(outT_b[:, bass.ds(p, 1), it * P:(it + 1) * P], bank[:, 6, 0:P].unsqueeze(1), a_ob)
                if it in (0, 2) and (slot is None or slot < NB * NU - T):
                    piece(pg + 1, 1 - k, (K, None, V)[it])
                if it == 3 and (slot is None or slot < NB * NU - 2 * T):
                    piece(pg + 2, k, Q)

            pg_row = [0]
            for b in range(NB):
                pg_row[0] = b * NP
                for it in range(T):
                    unit(b * NP, 0, it, b * NU + it)
                with act.Fori(0, B_LOOPS) as r:
                    for k in (1, 0):
                        for it in range(T):
                            unit(r * 2 + (b * NP + 2 - k), k, it)
                for p in range(2 * B_LOOPS + 1, NP):
                    for it in range(T):
                        unit(b * NP + p, p % 2, it, b * NU + p * T + it)

            for b in range(NB):
                act.wait_ge(pe_m, 2 * b + 1)
                copy(x2T[:, b * S:(b + 1) * S], bank[:, X2T_BANKS[b], :], a_m)
            act.wait_ge(v_m, 2)
            act.activation(ex[:], lg[:], ACT.Exp).then_inc(a_m, 1)
            act.wait_ge(v_m, 10)

            def scaled_parts(t):
                act.wait_ge(pe_y, t + 1)
                if t >= 3:
                    act.wait_ge(v_fin, 2 * (t - 3) + 1)
                for e in range(4):
                    act.activation(parts[t % 3][:, e, :], bank[:, EXPERT_BANKS[t % 3] + 1, e * E:(e + 1) * E], ACT.Copy,
                                   scale=coef[:, t, 4 + e:5 + e]).then_inc(a_part, 1)

            scaled_parts(0)
            act.wait_ge(pe_m, 6)
            for b in range(NB):
                copy(coefT[:, b * S:(b + 1) * S], bank[0:NE, 4 + b, :], a_m)
            for t in range(1, TT):
                scaled_parts(t)

        @block.tensor
        def _(pe):
            def transpose_to(out, in_, k=P):
                return pe.transpose(out, in_, ident[0:k, 0:k])

            def add_xbo(n):
                return pe.matmul(bank[:, n, :], ones_row[:], xbo_row[:].unsqueeze(1).broadcast_to([1, T, E]),
                                 start=False, stop=True, skip_group_check=True)

            pe.wait_ge(ld_rel, 16)
            pe.wait_ge(g_const, 2)
            for c in range(REL // P):
                last = transpose_to(bank[0:HD, 0, c * P:(c + 1) * P], rel_sb[:, c, :])
            last.then_inc(pe_set, 1)

            def setup(n):
                if n == 0:
                    pe.wait_ge(ld_b, 16 * N_LOADS_B)
                    pe.wait_ge(v_prep, 6)
                else:
                    pe.wait_ge(a_set, n + 4)
                if n < 2:
                    for e in range(4):
                        last = transpose_to(bank[:, 7, e * E:(e + 1) * E], we_sb[:, 4 * n + e, :])
                else:
                    last = transpose_to(bank[:, 7, 0:NB * M], ctx_sb[:], NB * M)
                last.then_inc(pe_set, 1)

            def prep_x(b):
                pe.wait_ge(ld_x[b], 16)
                for t in range(T):
                    last = transpose_to(bank[:, 7, t * P:(t + 1) * P], x_sb[b][:, t, :])
                last.then_inc(pe_prep, 1)

            def prep(b, j, n):
                if j < 2:
                    pe.matmul(bank[:, n, :], wqkv[:, j, :], xT[:], start=True, stop=True).then_inc(pe_prep, 1)
                else:
                    for t in range(T):
                        last = pe.matmul(bank[:, n, t * E:(t + 1) * E], xT[:, t * P:(t + 1) * P], wqkv[:, 2, :],
                                         start=True, stop=True)
                    last.then_inc(pe_prep, 1)

            def scores_a(gg, t):
                b, g = gg // G, gg % G
                if t == 0:
                    pe.wait_ge(g_build, 2 * (gg + 1))
                if g == 0 and t == 0:
                    pe.wait_ge(v_prep, b * 3 + 2)
                if gg == 0 and t == 0:
                    pe.wait_ge(ld_toep, 16 * QI)
                if gg > 0:
                    pe.wait_ge(a_expa, GT * (gg - 1) + t + 1)
                n = GI * (g + 1)
                q0 = GI * g + QI * t
                tile = slice(QI * t, QI * (t + 1))
                near = max(0, q0 - REL)
                if near:
                    pe.matmul(bank[:, t, 0:near], q_heads[gg % 2][:, tile, :], kT[b][:, 0:near], start=True, stop=True)
                pe.matmul(bank[:, t, near:n], q_heads[gg % 2][:, tile, :], kT[b][:, near:n], start=True, stop=False)
                pe.matmul(bank[:, t, near:n], q_pos[gg % 2][:, tile, :], toep[:, WIN - q0 + near:WIN - q0 + n],
                          start=False, stop=True).then_inc(pe_sa, 1)

            def evacuated(n):
                pe.wait_ge((v_eva, a_eva)[n % 2], n // 2 + 1)

            def transposes_a(gg, c):
                g = gg % G
                n = gg // G * NTR + TR0[g] + c
                if c == 0:
                    pe.wait_ge(v_na, GT * (gg + 1))
                if gg == 0 and c == 0:
                    pe.wait_ge(a_prep, 1)
                    pe.wait_ge(v_prep, 3)
                if n >= 2:
                    evacuated(n - 2)
                rows_n = min(P, GI * (g + 1) - P * c)
                for t in range(GT):
                    last = transpose_to(bank[0:rows_n, 4 + n % 2, t * P:(t + 1) * P],
                                        prob_a[gg % 2][:, t, c * P:c * P + rows_n])
                last.then_inc(pe_tra, 1)

            def pv_a(gg, c):
                b, g = gg // G, gg % G
                evacuated(b * NTR + TR0[g] + c)
                if c == 0 and gg > 0:
                    pe.wait_ge(v_oa, 2 * (gg - 1) + 1)
                if gg == G and c == 0:
                    pe.wait_ge(v_prep, 6)
                rows_n = min(P, GI * (g + 1) - P * c)
                for q in range(4):
                    moving = probT_a[0:rows_n, c, :].rearrange("p (i h) -> p i h", h=H)[:, :, 4 * q:4 * q + 4]
                    last = pe.matmul(bank[32 * q:32 * q + 32, 6, 0:P], v_sb[b][0:rows_n, c, 32 * q:32 * q + 32],
                                     moving, start=(c == 0), stop=(c == chunks(g) - 1),
                                     tile_position=(0, 32 * q))
                if c == chunks(g) - 1:
                    last.then_inc(pe_pva, 1)

            def wo_a(b):
                pe.wait_ge(v_oa, 2 * G * (b + 1))
                for t in range(T):
                    last = pe.matmul(bank[:, 7, t * E:(t + 1) * E], outT_a[b][:, t * P:(t + 1) * P], wo_sb[:],
                                     start=True, stop=True)
                last.then_inc(pe_wo, 1)

            def xn_transposes(b):
                pe.wait_ge(v_ln, LN * (2 * b + 2))
                for t in range(T):
                    last = transpose_to(bank[:, 7, t * P:(t + 1) * P], x1n[:, t, :])
                last.then_inc(pe_xn, 1)

            def project(pg, k, row, j, n):
                if isinstance(pg, int) and pg < FIRST_SPLIT:
                    pe.matmul(bank[:, n, :], w_pair[k][:, j, :], xnT[row][:], start=True, stop=True).then_inc(pe_pj, 1)
                    return
                if j == 0:
                    pe.wait_ge(g_ws, pg - 1)
                    pe.wait_ge(g_xs, row + 1)
                pe.matmul(bank[:, n, :], w_high[k][:, j, :], xn_high[row], start=True, stop=False)
                pe.matmul(bank[:, n, :], w_high[k][:, j, :], xn_low[row], start=False, stop=False)
                pe.matmul(bank[:, n, :], w_low[k][:, j, :], xn_high[row], start=False, stop=True).then_inc(pe_pj, 1)

            def piece(pg, k, row, j, n=7, tiles=range(T)):
                first = isinstance(pg, int) and pg == 0
                if j == MEM:
                    memories = ctxT[:, row * M:(row + 1) * M]
                    pe.matmul(bank[:, n, 2 * P:2 * P + M], w_pair[k][:, 3, :], memories, start=True, stop=True)
                    pe.matmul(bank[0:M, n, 3 * P:4 * P], memories, w_pair[k][:, 3, :], start=True,
                              stop=True).then_inc(pe_pj, 1)
                if j == Q:
                    if not first:
                        pe.wait_ge(a_pj, pg * A_PJ)
                    pe.wait_ge(ld_pair[k], pg * 32 + (2 - k) * 32)
                    project(pg, k, row, 0, n)
                if j == K:
                    pe.wait_ge(a_pj, pg * A_PJ + A_Q)
                    project(pg, k, row, 1, n)
                if j == V:
                    if tiles[0] == 0:
                        pe.wait_ge(a_pj, pg * A_PJ + A_K)
                    for t in tiles:
                        last = pe.matmul(bank[:, n, t * P:(t + 1) * P], xnT[row][:, t * P:(t + 1) * P],
                                         w_pair[k][:, 2, :], start=True, stop=True)
                    if tiles[-1] == T - 1:
                        last.then_inc(pe_pj, 1)

            def scores_b(pg, k, it, h, u=None):
                if h == 0 and u is not None:
                    pe.wait_ge(a_expb, u * 2 + 1)
                if it == 0 and h == 0:
                    pe.wait_ge(v_pj, pg * V_PJ + V_PJ)
                    pe.wait_ge(g_pj, pg * G_PJ + G_PJ)
                for c in range(2):
                    for q in (q_high, q_low):
                        last = pe.matmul(bank[:, 2 * h + c, 0:KH], q[k][:, h, it * P:(it + 1) * P],
                                         k_split[k][:, h, c * KH:(c + 1) * KH], start=(q is q_high), stop=(q is q_low))
                last.then_inc(pe_sb, 1)

            prep_x(0)
            pe.wait_ge(v_prep, 1)
            pe.wait_ge(ld_q, 2 * 16)
            prep(0, 0, 4)
            pe.wait_ge(ld_a, 16 * N_LOADS_A)
            pe.wait_ge(g_const, 10)
            pe.matmul(bank[:, 1, 0:1], rel0_row[:].rearrange("a h d -> a (h d)"), ones_row[:, 0:1], start=True, stop=True)
            prep(0, 1, 5)
            prep(0, 2, 6)
            pe.wait_ge(a_set, 4)
            for t in range(GT):
                scores_a(0, t)
            for gg in range(NB * G):
                if gg == PREP_1[0]:
                    prep_x(1)
                if gg == PREP_1[1]:
                    pe.wait_ge(v_prep, 4)
                    prep(1, 0, 7)
                if gg == PREP_1[2]:
                    pe.wait_ge(a_prep, 2)
                    prep(1, 1, 7)
                if gg == PREP_1[3]:
                    pe.wait_ge(v_prep, 5)
                    prep(1, 2, 7)
                if gg in SETUP:
                    setup(SETUP.index(gg))
                if gg == WO_0:
                    pe.wait_ge(a_set, 7)
                    wo_a(0)
                if gg == XN_0:
                    xn_transposes(0)
                if gg in PIECES_0:
                    if gg == PIECES_0[0]:
                        pe.wait_ge(a_xn, 1)
                    if gg == PIECES_0[MEM]:
                        pe.wait_ge(a_pj, A_Q)
                    if gg == PIECES_0[K]:
                        pe.wait_ge(v_pj, V_MEM)
                    piece(0, 0, 0, PIECES_0.index(gg))
                if gg == Q_1:
                    piece(1, 1, 0, Q)
                if gg + 1 < NB * G:
                    scores_a(gg + 1, 0)
                if gg > 0:
                    pv_a(gg - 1, chunks((gg - 1) % G) - 1)
                if gg == NB * G - 1:
                    pe.wait_ge(v_set, 8)
                    pe.wait_ge(a_expa, NB * G * GT)
                for t in range(GT):
                    if gg + 1 < NB * G and t < GT - 1:
                        scores_a(gg + 1, t + 1)
                    if gg == NB * G - 1 and t < 2:
                        scores_b(0, 0, 0, t)
                    if t < chunks(gg % G):
                        transposes_a(gg, t)
                    if 1 <= t < chunks(gg % G):
                        pv_a(gg, t - 1)
            pv_a(NB * G - 1, chunks(G - 1) - 1)

            def wo_b(pairs, tiles):
                for p in pairs:
                    for t in tiles:
                        pe.matmul(bank[:, 7, t * E:(t + 1) * E], outT_b[:, p, t * P:(t + 1) * P],
                                  xwo_sb[:, p, :], start=(p == 0 and t == 0), stop=False, skip_group_check=True)

            def unit(pg, k, row, it, slot=None):
                u = pg * 4 + it

                def next_scores(h):
                    if it < T - 1:
                        scores_b(pg, k, it + 1, h, u)
                    elif slot != NB * NU - 1:
                        scores_b(pg + 1, 1 - k, 0, h, u)

                next_scores(0)
                for h in range(2):
                    if slot == 0 and h == 0:
                        evacuated(NB * NTR - 2)
                        evacuated(NB * NTR - 1)
                        pe.wait_ge(v_oa, 2 * NB * G)
                    pe.wait_ge((g_nb, v_nb)[h], u + 1)
                    if h == 1 and slot != 0:
                        pe.wait_ge(a_ob, u)
                    stand_alone(pe, "pe")
                    for c in range(T):
                        last = transpose_to(bank[:, 4 + h, c * P:(c + 1) * P], prob_b[it % 2][:, h, TOKENS[h].start + c * P:TOKENS[h].start + (c + 1) * P])
                    if h == 1 and it == 0 and (slot is None or slot < NB * NU - T):
                        piece(pg + 1, 1 - k, (slot + T) // NU if slot is not None else row, MEM, 6)
                    if h == 1:
                        last = transpose_to(bank[0:2 * M, 6, P:2 * P], prob_b[it % 2][:].rearrange("p h n -> p (h n)")[:, S:S + 2 * M])
                    last.then_inc(pe_trb, 1)
                    if slot == 0 and h == 0:
                        pe.wait_ge(a_pj, A_PJ + A_Q)
                        wo_a(1)
                    if slot == NU and h == 1:
                        pe.wait_ge(a_pj, (NP + 1) * A_PJ + A_Q)
                        pe.wait_ge(a_ob, NU)
                        for t in range(T):
                            for p in range(NP):
                                last = pe.matmul(bank[:, 7, t * E:(t + 1) * E], outT_b[:, p, t * P:(t + 1) * P],
                                                 xwo_sb[:, p, :], start=(p == 0), stop=(p == NP - 1))
                        last.then_inc(pe_wob, 1)
                next_scores(1)
                if slot == 0:
                    pe.wait_ge(v_za, 2)
                if slot == NU:
                    pe.wait_ge(v_zb, 1)
                def ahead(n):
                    return row if slot is None else (slot + n * T) // NU

                def q_of_next():
                    if it == T - 1 and (slot is None or slot < NB * NU - 2 * T):
                        piece(pg + 2, k, ahead(2), Q)

                if slot == 3:
                    pe.wait_ge(a_pj, 2 * A_PJ)
                    xn_transposes(1)
                else:
                    q_of_next()
                if slot is None or slot < NB * NU - T:
                    if it < T - 1:
                        piece(pg + 1, 1 - k, ahead(1), (K, V, V)[it], tiles=range(2 * it - 2, 2 * it) if it else ())
                else:
                    if it == 0:
                        pe.wait_ge(a_pj, NB * NP * A_PJ)
                        pe.wait_ge(a_ob, u)
                    wo_b(range(NP - 1), (it, ))
                pe.wait_ge(v_evb, u + 1)
                pe.wait_ge(v_evm, u + 1)
                pe.wait_ge(a_evb, u + 1)
                if it == 0:
                    pe.wait_ge(a_pj, pg * A_PJ + A_PJ)
                    if slot is None or slot < NB * NU - T:
                        pe.wait_ge(v_pj, (pg + 1) * V_PJ + V_MEM)
                pe.matmul(bank[:, 6, 0:P], vm_pair[k][:], probTm[:], start=True, stop=False, skip_group_check=True)
                for c in range(T):
                    for h in range(2):
                        last = pe.matmul(bank[OWN[h], 6, 0:P], v_pair[k][:, c, OWN[h]], probT_b[h][:, c, :],
                                         start=False, stop=(c == T - 1), tile_position=(0, XD * h), skip_group_check=True)
                last.then_inc(pe_pvb, 1)
                if slot == 3:
                    pe.wait_ge(a_xn, 2)
                    q_of_next()

            for b in range(NB):
                for it in range(T):
                    unit(b * NP, 0, b, it, b * NU + it)
                with pe.Fori(0, B_LOOPS) as r:
                    for k in (1, 0):
                        for it in range(T):
                            unit(r * 2 + (b * NP + 2 - k), k, b, it)
                for p in range(2 * B_LOOPS + 1, NP):
                    for it in range(T):
                        unit(b * NP + p, p % 2, b, it, b * NU + p * T + it)

            pe.wait_ge(a_ob, NB * NU)
            wo_b((NP - 1, ), range(T))
            add_xbo(7).then_inc(pe_wob, 1)

            def experts(t):
                if t >= 3:
                    pe.wait_ge(v_acc, 4 * (t - 2))
                    pe.wait_ge(a_part, 4 * (t - 2))
                for c in range(2):
                    last = pe.matmul(bank[:, EXPERT_BANKS[t % 3] + c, :], x2T[:, t * P:(t + 1) * P],
                                     weT[:, 4 * c:4 * c + 4, :].rearrange("p e f -> p (e f)"), start=True, stop=True)
                last.then_inc(pe_y, 1)

            for b in range(NB):
                pe.wait_ge(v_ln, (len(LNS) - 1 + b) * LN)
                for t in range(T):
                    last = transpose_to(bank[:, X2T_BANKS[b], t * P:(t + 1) * P], x2[:, b * T + t, :])
                last.then_inc(pe_m, 1)
                pe.wait_ge(a_m, b + 1)
                for t in range(b * T, (b + 1) * T):
                    last = pe.matmul(bank[:, 4, t * NE:(t + 1) * NE], x2T[:, t * P:(t + 1) * P], wg_sb[:],
                                     start=True, stop=True)
                last.then_inc(pe_m, 1)
                experts(b)

            pe.wait_ge(v_m, 8)
            pe.wait_ge(g_const, 17)
            for t in range(TT - 1):
                pe.matmul(bank[:, 5, (t + 1) * NE:TT * NE], ones_bf[:],
                          chosen_bf[:, t:t + 1, :].broadcast_to([P, TT - 1 - t, NE]),
                          start=(t == 0), stop=False, skip_group_check=True)
            pe.matmul(bank[:, 5, 0:TT * NE], before[:], chosen_bf[:].rearrange("p t e -> p (t e)"),
                      start=False, stop=True, skip_group_check=True).then_inc(pe_m, 1)
            pe.wait_ge(v_zb, NB)
            experts(2)
            pe.wait_ge(v_m, 10)
            for t in range(TT):
                last = transpose_to(bank[0:NE, 4 + t // 4, (t % 4) * P:(t % 4 + 1) * P], coef[:, t, :])
            last.then_inc(pe_m, 1)
            experts(3)
            pe.wait_ge(a_m, 5)
            for t in range(TT):
                last = pe.matmul(bank[:, 4 + t // 4, (t % 4) * P:(t % 4 + 1) * P], coefT[:, t * P:(t + 1) * P],
                                 be_sb[:], start=True, stop=True)
            last.then_inc(pe_m, 1)
            for t in range(4, TT):
                experts(t)

        @block.vector
        def _(dve):
            dve.wait_ge(ld_q, 2 * 16)
            dve.tensor_scalar(bcols[:, 4:5], bcols[:, 0:1], SCALE_A, None, ALU.mult).then_inc(v_set, 1)
            dve.wait_ge(g_const, 5)
            dve.tensor_reduce(quad_mask[:], head_mask[:].rearrange("p (c q) -> p q c", q=4), AX.X,
                              ALU.add).then_inc(v_set, 1)

            def prep_x(b):
                dve.wait_ge(pe_prep, b * 4 + 1)
                dve.tensor_copy(xT[:], bank[:, 7, :]).then_inc(v_prep, 1)

            def prep_k(b, n):
                dve.wait_ge(pe_prep, b * 4 + 3)
                if b == 0:
                    dve.wait_ge(ld_a, 16 * N_LOADS_A)
                    dve.tensor_tensor(bcols[:, 5:6], bank[:, 1, 0:1], bcols[:, 1:2], ALU.add).then_inc(v_bias, 1)
                    dve.wait_ge(v_bias, 1)
                dve.tensor_scalar(kT[b][:], bank[:, n, :], bcols[:, 5:6], None, ALU.add).then_inc(v_prep, 1)

            def prep_v(b, n):
                dve.wait_ge(pe_prep, b * 4 + 4)
                dve.tensor_tensor(v_sb[b][:], bank[:, n, :].rearrange("p (t e) -> p t e", e=E),
                                  bias_rows[:, 0:1, :].broadcast_to([P, T, E]), ALU.add).then_inc(v_prep, 1)

            def max_a(gg, t):
                dve.wait_ge(pe_sa, GT * gg + t + 1)
                dve.tensor_reduce(stat_a[:, 0, gg % 2, t:t + 1], bank[:, t, 0:GI * (gg % G + 1)], AX.X, ALU.max,
                                  negate=True).then_inc(v_maxa, 1)

            def normalise_a(gg, t):
                dve.wait_ge(a_expa, GT * gg + t + 1)
                dve.reciprocal(stat_a[:, 2, gg % 2, t:t + 1], stat_a[:, 1, gg % 2, t:t + 1]).then_inc(v_rca, 1)
                dve.wait_ge(v_rca, GT * gg + t + 1)
                row = prob_a[gg % 2][:, t, 0:GI * (gg % G + 1)]
                dve.tensor_scalar(row, row, stat_a[:, 2, gg % 2, t:t + 1], None, ALU.mult).then_inc(v_na, 1)

            def ln_begin(i, src):
                v0 = LN * i
                for t in range(T):
                    dve.bn_stats(stats[:, t, :], src[:, t, :]).then_inc(v_ln, 1)
                for t in range(T):
                    dve.wait_ge(v_ln, v0 + t + 1)
                    dve.bn_aggr(moments[:, t, :], stats[:, t, :]).then_inc(v_ln, 1)
                dve.wait_ge(v_ln, v0 + 2 * T)
                dve.tensor_scalar(var_eps[:, 0:T], moments[:, 0:T, 1], EPS, None, ALU.add).then_inc(v_ln, 1)

            def ln_apply(i, src, out):
                dve.wait_ge(g_pow, i + 1)
                for t in range(T):
                    dve.tensor_scalar(out[:, t, :], src[:, t, :], moments[:, t, 0:1], rstd[:, t:t + 1],
                                      ALU.subtract, ALU.mult).then_inc(v_ln, 1)
                dve.wait_ge(v_ln, LN * (i + 1))

            def row_tiles(tile, b):
                return tile[:, b * T:(b + 1) * T, :]

            def residual_a(b):
                dve.wait_ge(g_bias, b + 1)
                dve.wait_ge(pe_wo, b + 1)
                dve.tensor_tensor(row_tiles(z, b), bank[:, 7, :].rearrange("p (t e) -> p t e", e=E), x_sb[b][:],
                                  ALU.add).then_inc(v_za, 1)
                dve.wait_ge(v_za, b + 1)

            def residual_b(b):
                if b == 0:
                    dve.wait_ge(g_bias, 3)
                dve.wait_ge(pe_wob, b + 1)
                dve.tensor_tensor(row_tiles(z, b), bank[:, 7, :].rearrange("p (t e) -> p t e", e=E), x1[b][:],
                                  ALU.add).then_inc(v_zb, 1)
                dve.wait_ge(v_zb, b + 1)

            def piece(pg, k, j, n=7):
                if j == MEM:
                    dve.wait_ge(pe_pj, pg * 4 + 2)
                    for h in range(2):
                        dve.tensor_copy(k_split[k][OWN[h], h, MEMORIES[h]], bank[OWN[h], n, 2 * P:2 * P + M]).then_inc(v_pj, 1)
                    for h in range(2):
                        dve.tensor_copy(vm_pair[k][M * h:M * (h + 1), OWN[h]],
                                        bank[0:M, n, 3 * P + XD * h:3 * P + XD * (h + 1)]).then_inc(v_pj, 1)
                    dve.wait_ge(v_pj, pg * V_PJ + 2)
                    stand_alone(dve, "dve")
                    for h in range(2):
                        dve.tensor_tensor(k_split[k][OTHER[h], h, MEMORIES[h]], bank[OWN[h], n, 2 * P:2 * P + M],
                                          k_split[k][OWN[h], h, MEMORIES[h]].bitcast(F32), ALU.subtract).then_inc(v_pj, 1)
                if j == Q:
                    dve.wait_ge(a_pj, pg * A_PJ + 1)
                    for h in range(2):
                        dve.tensor_copy(q_high[k][OTHER[h], h, :], q_raw[OWN[h], :]).then_inc(v_pj, 1)

            def max_b(u, h):
                dve.wait_ge(pe_sb, u * 2 + (h + 1))
                dve.tensor_reduce(stat_b[:, 0, h:h + 1], bank[:, 2 * h:2 * h + 2, 0:KH], AX.XY, ALU.max,
                                  negate=True).then_inc(v_maxb, 1)

            def recip_b(u, h, i):
                dve.wait_ge(a_expb, u * 2 + (h + 1))
                dve.reciprocal(stat_b[:, 2, h:h + 1], stat_b[:, 1, h:h + 1]).then_inc(v_rcb, 1)
                if h == 1:
                    dve.wait_ge(v_rcb, u * 2 + 2)
                    stand_alone(dve, "dve")
                    dve.tensor_scalar(prob_b[i][:, 1, :], prob_b[i][:, 1, :], stat_b[:, 2, 1:2], None, ALU.mult).then_inc(v_nb, 1)

            def take_out(gg):
                b, g = gg // G, gg % G
                dve.wait_ge(pe_pva, gg + 1)
                dve.tensor_tensor(o_masked[:], bank[:, 6, 0:P].rearrange("p (i q) -> p i q", q=4),
                                  quad_mask[:].unsqueeze(1).broadcast_to([P, GI, 4]), ALU.mult).then_inc(v_oa, 1)
                dve.wait_ge(v_oa, 2 * gg + 1)
                dve.tensor_reduce(outT_a[b][:, GI * g:GI * (g + 1)], o_masked[:], AX.X, ALU.add).then_inc(v_oa, 1)

            prep_x(0)
            prep_k(0, 5)
            prep_v(0, 6)
            for k in range(2):
                for h in range(2):
                    dve.memset(q_low[k][OTHER[h], h, :].bitcast(F32), 0.0).then_inc(v_set, 1)
                dve.memset(vm_pair[k][:], 0.0).then_inc(v_set, 1)
            for t in range(GT):
                max_a(0, t)
            for t in range(GT):
                normalise_a(0, t)
            for gg in range(NB * G):
                b, g = gg // G, gg % G
                if gg == PREP_1[0]:
                    prep_x(1)
                if gg == PREP_1[2]:
                    prep_k(1, 7)
                if gg == PREP_1[3]:
                    prep_v(1, 7)
                if gg == WO_0:
                    residual_a(0)
                if gg == LN_0:
                    ln_begin(0, row_tiles(z, 0))
                if gg == APPLY_0:
                    ln_apply(0, row_tiles(z, 0), x1[0])
                if gg == LN_1:
                    ln_begin(1, x1[0])
                if gg == APPLY_1:
                    ln_apply(1, x1[0], x1n)
                if gg == PIECES_0[MEM]:
                    piece(0, 0, MEM)
                    piece(0, 0, Q)
                if gg + 1 < NB * G:
                    max_a(gg + 1, 0)
                else:
                    max_b(0, 0)
                for t in range(GT):
                    if gg + 1 < NB * G and t < GT - 1:
                        max_a(gg + 1, t + 1)
                    if t == 0 and gg > 0:
                        take_out(gg - 1)
                    n = b * NTR + TR0[g] + t
                    if t < chunks(g) and n % 2 == 0:
                        rows_n = min(P, GI * (g + 1) - P * t)
                        dve.wait_ge(pe_tra, n + 1)
                        dve.tensor_copy(probT_a[0:rows_n, t, :], bank[0:rows_n, 4, :]).then_inc(v_eva, 1)
                    if gg + 1 < NB * G:
                        normalise_a(gg + 1, t)
                    elif t == 0:
                        max_b(0, 1)
                    elif t < 3:
                        recip_b(0, t - 1, 0)
            take_out(NB * G - 1)

            def unit(pg, k, it, slot=None):
                u = pg * 4 + it
                last = slot == NB * NU - 1
                projects = slot is None or slot < NB * NU - T
                if not last:
                    max_b(u + 1, 0)
                dve.wait_ge(pe_trb, u * 2 + 1)
                dve.tensor_copy(probT_b[0][:], bank[:, 4, :].rearrange("p (c n) -> p c n", n=P)).then_inc(v_evb, 1)
                if slot == 0:
                    residual_a(1)
                if slot == NU:
                    residual_b(0)
                dve.wait_ge(pe_trb, u * 2 + 2)
                dve.tensor_copy(probTm[:], bank[0:2 * M, 6, P:2 * P]).then_inc(v_evm, 1)
                if projects and it == 0:
                    piece(pg + 1, 1 - k, MEM, 6)
                if not last:
                    max_b(u + 1, 1)
                if not last:
                    recip_b(u + 1, 0, 1 - it % 2)
                    recip_b(u + 1, 1, 1 - it % 2)
                if projects and it == 1:
                    piece(pg + 1, 1 - k, Q)
                if slot in SPLIT_XN:
                    b = SPLIT_XN.index(slot)
                    dve.wait_ge(g_build, 2 * NB * G)
                    dve.wait_ge(a_xn, b + 1)
                    dve.tensor_copy(xn_high[b], xnT[b][:]).then_inc(v_xs, 1)
                if it == 2 and (slot is None or slot < NB * NU - 2 * T):
                    dve.wait_ge(ld_pair[k], pg * 32 + (4 - k) * 32)
                    dve.tensor_copy(w_high[k], w_pair[k][:, 0:2, :]).then_inc(v_ws, 1)
                if slot == 0:
                    ln_begin(2, row_tiles(z, 1))
                if slot == 1:
                    ln_apply(2, row_tiles(z, 1), x1[1])
                    ln_begin(3, x1[1])
                if slot == 2:
                    ln_apply(3, x1[1], x1n)
                if slot == NU:
                    ln_begin(4, row_tiles(z, 0))
                if slot == NU + 2:
                    ln_apply(4, row_tiles(z, 0), row_tiles(x2, 0))

            for b in range(NB):
                for it in range(T):
                    unit(b * NP, 0, it, b * NU + it)
                with dve.Fori(0, B_LOOPS) as r:
                    for k in (1, 0):
                        for it in range(T):
                            unit(r * 2 + (b * NP + 2 - k), k, it)
                for p in range(2 * B_LOOPS + 1, NP):
                    for it in range(T):
                        unit(b * NP + p, p % 2, it, b * NU + p * T + it)

            residual_b(1)
            ln_begin(5, row_tiles(z, 1))
            ln_apply(5, row_tiles(z, 1), row_tiles(x2, 1))

            def step(ins, n):
                ins.then_inc(v_m, 1)
                dve.wait_ge(v_m, n)

            def over_experts(col):
                return tok[:, col, :].unsqueeze(2).broadcast_to([P, TT, NE])

            dve.wait_ge(pe_m, 4)
            logits = bank[:, 4, 0:TT * NE].rearrange("p (t e) -> p t e", e=NE)
            step(dve.tensor_reduce(tok[:, 0, :], logits, AX.X, ALU.max), 1)
            step(dve.tensor_tensor(lg[:], logits, over_experts(0), ALU.subtract), 2)
            dve.wait_ge(a_m, 3)
            step(dve.tensor_reduce(tok[:, 1, :], ex[:], AX.X, ALU.max), 3)
            step(dve.tensor_tensor(cand[:], ex[:], over_experts(1), ALU.is_ge), 4)
            dve.wait_ge(g_const, 17)
            step(dve.tensor_tensor(cand[:], cand[:], rank[:].unsqueeze(1).broadcast_to([P, TT, NE]), ALU.mult), 5)
            step(dve.tensor_reduce(tok[:, 4, :], cand[:], AX.X, ALU.max), 6)
            step(dve.tensor_tensor(chosen[:], cand[:], over_experts(4), ALU.is_equal), 7)
            step(dve.tensor_copy(chosen_bf[:], chosen[:]), 8)
            dve.tensor_reduce(tok[:, 2, :], ex[:], AX.X, ALU.add).then_inc(v_gate, 1)
            dve.wait_ge(v_gate, 1)
            dve.reciprocal(tok[:, 2, :], tok[:, 2, :]).then_inc(v_gate, 1)
            dve.wait_ge(v_gate, 2)
            dve.tensor_tensor(tok[:, 3, :], tok[:, 1, :], tok[:, 2, :], ALU.mult).then_inc(v_gate, 1)
            dve.wait_ge(v_gate, 3)
            dve.wait_ge(pe_m, 5)
            places = bank[:, 5, 0:TT * NE].rearrange("p (t e) -> p t e", e=NE)
            step(dve.scalar_tensor_tensor(out=coef[:], in0=places, scalar=float(CAP), in1=chosen[:],
                                          op0=ALU.is_lt, op1=ALU.mult), 9)
            step(dve.tensor_tensor(coef[:], coef[:], over_experts(3), ALU.mult), 10)

            def accumulate(t, e):
                if e == 0:
                    dve.wait_ge(pe_y, t + 1)
                else:
                    dve.wait_ge(v_acc, 4 * t + e)
                y = bank[:, EXPERT_BANKS[t % 3], e * E:(e + 1) * E]
                dve.scalar_tensor_tensor(out=z[:, t, :], in0=y, scalar=coef[:, t, e:e + 1],
                                         in1=(z if e else x2)[:, t, :], op0=ALU.mult,
                                         op1=ALU.add).then_inc(v_acc, 1)

            def finish(t, n):
                if n == 0:
                    dve.wait_ge(g_sum, 2 * (t + 1))
                    dve.wait_ge(v_acc, 4 * (t + 1))
                    dve.tensor_tensor(z[:, t, :], z[:, t, :], parts[t % 3][:, 0, :], ALU.add).then_inc(v_fin, 1)
                if n == 1:
                    dve.wait_ge(pe_m, 7)
                    dve.wait_ge(v_fin, 2 * t + 1)
                    dve.tensor_tensor(z[:, t, :], bank[:, 4 + t // 4, (t % 4) * P:(t % 4 + 1) * P], z[:, t, :],
                                      ALU.add).then_inc(v_fin, 1)
                if n == 2:
                    dve.wait_ge(v_fin, 2 * t + 2)
                    dve.bn_stats(stats[:, t, :], z[:, t, :]).then_inc(v_lnf, 1)

            def last_ln_begin(b):
                for t in range(b * T, (b + 1) * T):
                    dve.wait_ge(v_lnf, t + 1)
                    dve.bn_aggr(moments[:, t, :], stats[:, t, :]).then_inc(v_lnm, 1)
                dve.wait_ge(v_lnm, LN_MORE * b + T)
                dve.tensor_scalar(var_eps[:, b * T:(b + 1) * T], moments[:, b * T:(b + 1) * T, 1], EPS, None,
                                  ALU.add).then_inc(v_lnm, 1)

            def last_ln_apply(b):
                dve.wait_ge(g_powf, b + 1)
                for t in range(b * T, (b + 1) * T):
                    dve.tensor_scalar(y_out[:, t, :], z[:, t, :], moments[:, t, 0:1], rstd[:, t:t + 1],
                                      ALU.subtract, ALU.mult).then_inc(v_lnm, 1)

            for t in range(TT + 1):
                for e in range(4):
                    if t < TT:
                        accumulate(t, e)
                    if t > 0 and e < 3:
                        finish(t - 1, e)
                if t == T:
                    last_ln_begin(0)
                if t == TT - 1:
                    last_ln_apply(0)
            last_ln_begin(1)
            last_ln_apply(1)


_INS = ['x', 'ctx_1024', 'L0_attn_Wq', 'L0_attn_bq', 'L0_attn_Wk', 'L0_attn_bk', 'L0_attn_Wv', 'L0_attn_bv',
        'L0_attn_Wo', 'L0_attn_bo', 'L0_attn_rel_key', 'L0_xattn_ln_g', 'L0_xattn_ln_b', 'L0_xattn_Wq',
        'L0_xattn_Wkv', 'L0_xattn_Wm', 'L0_xattn_Wo', 'L0_xattn_bo', 'L0_ffn_wg', 'L0_ffn_W', 'L0_ffn_b']


def kernel(**inputs):
    import numpy as np
    import concourse.bacc as bacc
    from concourse.bass_utils import run_bass_kernel_spmd

    nc = bacc.Bacc("TRN2", target_bir_lowering=False, num_devices=1)
    arrays, args = {}, []
    for name in _INS:
        a = np.ascontiguousarray(inputs[name])
        arrays[f"in_{name}"] = a
        args.append(nc.dram_tensor(f"in_{name}", a.shape, mybir.dt.from_np(a.dtype), kind="ExternalInput").ap())
    out = nc.dram_tensor("out_x", (NB, S, E), F32, kind="ExternalOutput").ap()
    decoder_layer(nc, *args, out)
    return run_bass_kernel_spmd(nc, [arrays], core_ids=[0]).results[0]["out_x"]
```
